# Optimizing a Trainium2 kernel written in Bass

```python
import numpy as np
import jax
import jax.numpy as jnp

def _softmax(x, axis=-1):
    return jax.nn.softmax(x, axis=axis)

def _gelu(x):
    return jax.nn.gelu(x, approximate=True)

def _silu(x):
    return jax.nn.silu(x)

def _sigmoid(x):
    return jax.nn.sigmoid(x)

def _layernorm(x, axis=-1, eps=1e-05):
    m = jnp.mean(x, axis=axis, keepdims=True)
    v = jnp.var(x, axis=axis, keepdims=True)
    return (x - m) / jnp.sqrt(v + eps)

def _scatter_add(tgt, idx, src, axis=0):
    return tgt.at[idx].add(src)

def _segment_sum(src, seg, n):
    return jax.ops.segment_sum(src, seg, n)
kernel_name = 'mk_prb_d1_jaxref_r8_d592c9'

def setup_inputs(seed: int=0):
    np.random.seed(seed)
    _w = jnp.asarray

    def _L0_attn_setup():
        import jax, jax.numpy as jnp
        import numpy as np
        EMB, HEADS, HIDDEN = (128, 16, 64)
        BS, N = (2, 256)
        key = jax.random.key(seed)
        ks = jax.random.split(key, 7)
        s_in = 1.0 / np.sqrt(EMB)
        s_u = 1.0 / np.sqrt(HEADS * HIDDEN)
        return {'x': jax.random.normal(ks[0], (BS, N, EMB), dtype=jnp.float32), 'w_q': jax.random.uniform(ks[1], (EMB, HEADS * HIDDEN), jnp.float32, -s_in, s_in), 'w_k': jax.random.uniform(ks[2], (EMB, HEADS * HIDDEN), jnp.float32, -s_in, s_in), 'w_v': jax.random.uniform(ks[3], (EMB, HEADS * HIDDEN), jnp.float32, -s_in, s_in), 'w_u': jax.random.uniform(ks[4], (HEADS * HIDDEN, EMB), jnp.float32, -s_u, s_u), 'b_u': jax.random.uniform(ks[5], (EMB,), jnp.float32, -s_u, s_u)}
    _L0_attn_in = _L0_attn_setup()

    def _L0_ffn_setup():
        import jax, jax.numpy as jnp
        import numpy as np
        B, S, H, F, E, K = (4, 512, 128, 512, 8, 2)
        LN_EPS = 1e-05
        key = jax.random.key(seed)
        kx, kr, k1, k2 = jax.random.split(key, 4)
        x = jax.random.normal(kx, (B, S, H), dtype=jnp.float32)
        gamma = jnp.ones((H,), jnp.float32)
        beta = jnp.zeros((H,), jnp.float32)
        Wr = jax.random.normal(kr, (H, E), jnp.float32) * 0.02
        br = jnp.zeros((E,), jnp.float32)
        W1 = jax.random.normal(k1, (E, H, F), jnp.float32) * (1.0 / np.sqrt(H))
        b1 = jnp.zeros((E, F), jnp.float32)
        W2 = jax.random.normal(k2, (E, F, H), jnp.float32) * (1.0 / np.sqrt(F))
        b2 = jnp.zeros((E, H), jnp.float32)
        return {'x': x, 'gamma': gamma, 'beta': beta, 'Wr': Wr, 'br': br, 'W1': W1, 'b1': b1, 'W2': W2, 'b2': b2}
    _L0_ffn_in = _L0_ffn_setup()
    _d = {'L0_attn_x': _L0_attn_in['x'], 'L0_attn_w_q': _L0_attn_in['w_q'], 'L0_attn_w_k': _L0_attn_in['w_k'], 'L0_attn_w_v': _L0_attn_in['w_v'], 'L0_attn_w_u': _L0_attn_in['w_u'], 'L0_attn_b_u': _L0_attn_in['b_u'], 'L0_ffn_gamma': _L0_ffn_in['gamma'], 'L0_ffn_beta': _L0_ffn_in['beta'], 'L0_ffn_Wr': _L0_ffn_in['Wr'], 'L0_ffn_br': _L0_ffn_in['br'], 'L0_ffn_W1': _L0_ffn_in['W1'], 'L0_ffn_b1': _L0_ffn_in['b1'], 'L0_ffn_W2': _L0_ffn_in['W2'], 'L0_ffn_b2': _L0_ffn_in['b2']}
    _x0 = _d['L0_attn_x']
    _d['L0_attn_x'] = jax.random.normal(jax.random.fold_in(jax.random.key(seed), 1), (4, 1024, 128), dtype=_x0.dtype)
    del _x0
    return _d

def reference(L0_attn_x, L0_attn_w_q, L0_attn_w_k, L0_attn_w_v, L0_attn_w_u, L0_attn_b_u, L0_ffn_gamma, L0_ffn_beta, L0_ffn_Wr, L0_ffn_br, L0_ffn_W1, L0_ffn_b1, L0_ffn_W2, L0_ffn_b2):

    def _L0_attn_ref(x, w_q, w_k, w_v, w_u, b_u):
        import jax, jax.numpy as jnp
        import numpy as np
        EMB, HEADS, HIDDEN = (128, 16, 64)
        BS, N = (2, 256)
        bs, n, emb = x.shape
        h, hd = (HEADS, HIDDEN)
        q = (x @ w_q).reshape(bs, n, h, hd)
        k = (x @ w_k).reshape(bs, n, h, hd)
        v = (x @ w_v).reshape(bs, n, h, hd)
        scale = 1.0 / jnp.sqrt(jnp.asarray(hd, dtype=x.dtype))
        q = q * scale
        k = k * scale
        dot = jnp.einsum('bqhd,bkhd->bhqk', q, k)
        causal = jnp.tril(jnp.ones((n, n), dtype=bool))
        dot = jnp.where(causal, dot, jnp.asarray(-jnp.inf, dtype=dot.dtype))
        att = jax.nn.softmax(dot, axis=-1)
        out = jnp.einsum('bhqk,bkhd->bqhd', att, v).reshape(bs, n, h * hd)
        return out @ w_u + b_u

    def _L0_ffn_ref(x, gamma, beta, Wr, br, W1, b1, W2, b2):
        import jax, jax.numpy as jnp
        import numpy as np
        B, S, H, F, E, K = (4, 512, 128, 512, 8, 2)
        LN_EPS = 1e-05
        residual = x
        mu = jnp.mean(x, axis=-1, keepdims=True)
        var = jnp.var(x, axis=-1, keepdims=True)
        xn = (x - mu) * jax.lax.rsqrt(var + LN_EPS) * gamma + beta
        probs = jax.nn.softmax(xn @ Wr + br, axis=-1)
        scores, idx = jax.lax.top_k(probs, K)

        def expert_fn(w):
            W1_e, b1_e, W2_e, b2_e = w
            return jax.nn.relu(xn @ W1_e + b1_e) @ W2_e + b2_e
        full = jax.lax.map(expert_fn, (W1, b1, W2, b2))
        full = jnp.moveaxis(full, 0, 2)
        c = jnp.einsum('ef,efh->eh', jax.nn.relu(b1), W2) + b2
        c_total = c.sum(axis=0)
        sel_full = jnp.take_along_axis(full, idx[..., None], axis=2)
        c_sel = c[idx]
        output = jnp.sum(scores[..., None] * (sel_full - c_sel + c_total), axis=2)
        return residual + output
    x = L0_attn_x
    xn = _layernorm(x, axis=-1)
    x = x + _L0_attn_ref(xn, L0_attn_w_q, L0_attn_w_k, L0_attn_w_v, L0_attn_w_u, L0_attn_b_u) + _L0_ffn_ref(xn, L0_ffn_gamma, L0_ffn_beta, L0_ffn_Wr, L0_ffn_br, L0_ffn_W1, L0_ffn_b1, L0_ffn_W2, L0_ffn_b2)
    return x

_drawn_inputs = setup_inputs


def setup_inputs(seed=0):
    import zlib

    import numpy as np

    out = dict(_drawn_inputs(seed))
    spreads = {'L0_ffn_gamma': (1.0, 0.6),
     'L0_ffn_beta': (0.0, 0.413),
     'L0_ffn_br': (0.0, 0.1),
     'L0_ffn_b1': (0.0, 0.269),
     'L0_ffn_b2': (0.0, 0.27)}
    factors = {'L0_attn_w_q': 8.0,
     'L0_attn_w_k': 8.0,
     'L0_attn_w_v': 4.174,
     'L0_attn_w_u': 4.242,
     'L0_attn_b_u': 5.634}
    for name, (base, spread) in spreads.items():
        noise = np.random.default_rng([zlib.crc32(name.encode()), seed]).standard_normal(out[name].shape)
        drawn = base * np.exp(spread * noise) if base else spread * noise
        out[name] = jnp.asarray(drawn.astype(out[name].dtype))
    for name, factor in factors.items():
        out[name] = (out[name] * factor).astype(out[name].dtype)
    return out
```

```python
from contextlib import ExitStack

import concourse.bass as bass
from concourse import mybir

F32 = mybir.dt.float32
F32R = mybir.dt.float32r
BF16 = mybir.dt.bfloat16
ALU = mybir.AluOpType
ACT = mybir.ActivationFunctionType
AX = mybir.AxisListType

P = 128
LN_EPS = 1e-5
MASKED = -3.0e38


def build(nc, x, w_q, w_k, w_v, w_u, b_u, gamma, beta, w_r, b_r, w_1, b_1, w_2, b_2, out):
    NB, N, E = x.shape
    HD = 64
    H = w_q.shape[1] // HD
    NX, _, F = w_1.shape
    TOK = NB * N
    NT = TOK // P
    TB = N // P
    BLK = 512
    NG = TOK // BLK
    GB = N // BLK
    TG = BLK // P
    FB = F // P
    PAIRS = H // 2
    STEPS = NB * PAIRS
    SLOTS = 2 * TB
    QK_SCALE = 1.0 / HD
    assert E == P and N == 2 * BLK and F == BLK and NX == 8 and H % 2 == 0

    x_t = x.rearrange("b n e -> (b n) e").rearrange("(t p) e -> p t e", p=P)
    out_t = out.rearrange("b n e -> (b n) e").rearrange("(t p) e -> p t e", p=P)

    gate_dram = nc.dram_tensor("gate_rows", (NX * NT, P), F32).ap()
    gate_rows = gate_dram.rearrange("(e t) p -> e (t p)", e=NX)
    WQKV, WALL = 6, 10
    wsplit_dram = nc.dram_tensor("split_weights", (PAIRS, P, WALL * P), F32).ap()

    with ExitStack() as ctx:
        def sem(name):
            return ctx.enter_context(nc.semaphore(name))

        def sb(scope, name, shape, dt=F32):
            return scope.enter_context(nc.sbuf_tensor(name, shape, dt))

        ident = sb(ctx, "ident", [P, P])
        ident_bf = sb(ctx, "ident_bf", [P, P], BF16)
        causal = sb(ctx, "causal", [P, P], BF16)
        xnT_hi = sb(ctx, "xnT_hi", [P, TOK], F32R)
        xnT_lo = sb(ctx, "xnT_lo", [P, TOK], F32R)
        acc = sb(ctx, "acc", [P, TOK])

        early = ExitStack()
        x2T_hi = sb(early, "x2T_hi", [P, TOK], F32R)
        x2T_lo = sb(early, "x2T_lo", [P, TOK], F32R)
        ptab = sb(early, "ptab", [P, NX, FB + 1])

        setup = ExitStack()
        xs = sb(setup, "xs", [P, NT, P])
        xs2 = sb(setup, "xs2", [P, NT, P])
        sq = sb(setup, "sq", [P, NT, P])
        x2T = sb(setup, "x2T", [P, TOK])
        w2_all = sb(setup, "w2_all", [P, NX * FB, P])
        w_raw = sb(setup, "w_raw", [P, 3, H * HD])
        u_raw = sb(setup, "u_raw", [P, H, P])
        w_st = sb(setup, "w_st", [P, 2, PAIRS, 2, P], F32R)
        rows = sb(setup, "rows", [P, P])
        cols = sb(setup, "cols", [P, P])
        relu_b1 = sb(setup, "relu_b1", [P, NX * FB])
        b2_row, gamma_row, beta_row, bu_row = NX * FB, NX * FB + NX, NX * FB + NX + 1, NX * FB + NX + 2
        wr_sb = sb(setup, "wr_sb", [P, NX])
        br_sb = sb(setup, "br_sb", [P, NX])
        c_sum = sb(setup, "c_sum", [P, 2])
        c_all = sb(setup, "c_all", [P, NX])
        stat = sb(setup, "stat", [P, 2, 5, NT])
        logit = sb(setup, "logit", [P, NT, NX])
        prob = sb(setup, "prob", [P, NT, NX])
        r_stat = sb(setup, "r_stat", [P, 3, NT])
        rank = sb(setup, "rank", [P, NT, NX])
        beats = sb(setup, "beats", [P, 2, NT, NX])
        gate = sb(setup, "gate", [P, NX, NT])
        gateT = sb(setup, "gateT", [P, 2, P])
        setup.close()

        ffn = ExitStack()
        w_ffn = sb(ffn, "w_ffn", [P, 2, F])
        w1_hi = [sb(ffn, f"w1_hi{i}", [P, F], F32R) for i in range(2)]
        w1_lo = [sb(ffn, f"w1_lo{i}", [P, F], F32R) for i in range(2)]
        w2_hi = [sb(ffn, f"w2_hi{i}", [P, F], F32R) for i in range(2)]
        w2_lo = [sb(ffn, f"w2_lo{i}", [P, F], F32R) for i in range(2)]
        par = [sb(ffn, f"par{i}", [P, FB + 1]) for i in range(2)]
        g_bc = [sb(ffn, f"g_bc{i}", [P, TOK]) for i in range(2)]
        hid = sb(ffn, "hid", [P, FB, BLK])
        hid_hi = sb(ffn, "hid_hi", [P, 2, FB, BLK], F32R)
        hid_lo = sb(ffn, "hid_lo", [P, 2, FB, BLK], F32R)
        gated = sb(ffn, "gated", [P, BLK])
        ffn.close()
        early.close()

        att = ExitStack()
        w_qkv = sb(att, "w_qkv", [P, WQKV, P], F32R)
        w_out = sb(att, "w_out", [P, WALL - WQKV, P], F32R)
        q_st = sb(att, "q_st", [P, 2, N], F32R)
        k_st = sb(att, "k_st", [P, 2, N], F32R)
        v_st = sb(att, "v_st", [P, N])
        qq = [sb(att, f"qq{h}", [P, N], F32R) for h in range(2)]
        kh = [sb(att, f"kh{h}", [P, N], F32R) for h in range(2)]
        kl = [sb(att, f"kl{h}", [P, N], F32R) for h in range(2)]
        vv = sb(att, "vv", [P, TB, 2, P], F32R)
        prb = sb(att, "prb", [P, 4, N])
        pT_hi = [sb(att, f"pT_hi{g}", [P, TG * (g + 1), BLK], F32R) for g in range(GB)]
        pT_lo = [sb(att, f"pT_lo{g}", [P, TG * (g + 1), BLK], F32R) for g in range(GB)]
        o_1 = sb(att, "o_1", [P, 2, N], F32R)
        o_2 = sb(att, "o_2", [P, 2, N], F32R)
        nmax = sb(att, "nmax", [P, 4])
        rsum = sb(att, "rsum", [P, 4])
        rinv = sb(att, "rinv", [P, 4])
        spare = sb(att, "spare", [P, 2])
        res = sb(att, "res", [P, NT, P])
        att.close()

        ps = ctx.enter_context(nc.psum_tensor("ps", [P, 8, BLK], F32))

        phase = sem("phase")
        made = sem("made")
        ld_x = [sem(f"ld_x{c}") for c in range(NB)]
        ld_rows, ld_w2, ld_wr, ld_raw = sem("ld_rows"), sem("ld_w2"), sem("ld_wr"), sem("ld_raw")
        centred, squared, sd_done, rstd_done, normed = (
            sem("centred"), sem("squared"), sem("sd_done"), sem("rstd_done"), sem("normed"))
        dve_step = sem("dve_step")
        rowsT, rowsT_sb, b1_relu, corr = sem("rowsT"), sem("rowsT_sb"), sem("b1_relu"), sem("corr")
        xT_ready, xT_hi, xT_lo = sem("xT_ready"), sem("xT_hi"), sem("xT_lo")
        x2_ready, x2_f, x2_hi, x2_lo = sem("x2_ready"), sem("x2_f"), sem("x2_hi"), sem("x2_lo")
        routed, shifted, exped, gated_up, gT_ready, gT_sb, gT_out = (
            sem("routed"), sem("shifted"), sem("exped"), sem("gated_up"), sem("gT_ready"), sem("gT_sb"), sem("gT_out"))
        w_split, w_saved = sem("w_split"), [sem(f"w_saved{k}") for k in range(5)]
        ld_e, w_hi_done, w_lo_done = sem("ld_e"), sem("w_hi_done"), sem("w_lo_done")
        h_ready, h_relu, h_hi, h_lo = sem("h_ready"), sem("h_relu"), sem("h_hi"), sem("h_lo")
        y_ready, y_gated, y_added = sem("y_ready"), sem("y_gated"), sem("y_added")
        ld_qkv, ld_out = sem("ld_qkv"), sem("ld_out")
        aux_ready, aux_hi, aux_free = sem("aux_ready"), sem("aux_hi"), sem("aux_free")
        qk_in = [sem("qk_in_a"), sem("qk_in_b")]
        s_ready, max_done, exp_done, rec_done, norm_done = (
            sem("s_ready"), sem("max_done"), sem("exp_done"), sem("rec_done"), sem("norm_done"))
        t_ready, t_hi, t_free = sem("t_ready"), sem("t_hi"), sem("t_free")
        o_ready, o_hi, o_lo, o_dup = sem("o_ready"), sem("o_hi"), sem("o_lo"), sem("o_dup")
        ld_res, f_ready, f_done, stored = sem("ld_res"), sem("f_ready"), sem("f_done"), sem("stored")

        ENGINES = 5
        MADE = 7

        def meet(eng, k):
            eng.drain().then_inc(phase, 1)
            eng.wait_ge(phase, ENGINES * k)

        def chunks(i):
            return [(j, min(TG, i + 1 - j)) for j in range(0, i + 1, TG)]

        HEAD_CHUNKS = sum(len(chunks(i)) for i in range(TB))
        CHUNKS = 2 * HEAD_CHUNKS

        def chunk_no(s):
            return HEAD_CHUNKS * (s // TB) + sum(len(chunks(i)) for i in range(s % TB))

        AUX0 = 6
        AUX = 10
        Q0, Q1, VT0, VT1, Y0, Y1, K0, K1, V0, V1 = range(AUX)
        PV_AT = {1: (1, 1), TB - 3: (0, 0), TB + 1: (0, 1), 2 * TB - 3: (1, 0)}
        PV_NO = {s: k for k, s in enumerate(sorted(PV_AT))}
        PT_BANK, O_BANK, AUX_BANK = 4, 6, 7
        AHEAD = 3

        def score_view(m, i):
            b = 2 * (m % 2)
            if i < TG:
                return ps[:, b, 0:P * (i + 1)]
            return ps[:, b:b + 2, 0:P * (i + 1) // 2]

        def prob_view(m, i):
            v = prb[:, m % 4, 0:P * (i + 1)]
            return v if i < TG else v.rearrange("p (a n) -> p a n", a=2)

        block = ctx.enter_context(nc.Block())

        @block.sync
        def _(sp):
            for c in range(NB):
                sp.dma_start(xs[:, TB * c:TB * (c + 1), :], x_t[:, TB * c:TB * (c + 1), :]).then_inc(ld_x[c], 16)
            sp.wait_ge(made, 1)
            sp.dma_start(rows[0:b2_row, :], b_1.rearrange("e (f p) -> (e f) p", p=P)).then_inc(ld_rows, 16)
            sp.dma_start(rows[b2_row:gamma_row, :], b_2).then_inc(ld_rows, 16)
            sp.dma_start(rows[gamma_row:gamma_row + 1, :], gamma.rearrange("(a e) -> a e", a=1)).then_inc(ld_rows, 16)
            sp.dma_start(rows[beta_row:beta_row + 1, :], beta.rearrange("(a e) -> a e", a=1)).then_inc(ld_rows, 16)
            sp.dma_start(rows[bu_row:bu_row + 1, :], b_u.rearrange("(a e) -> a e", a=1)).then_inc(ld_rows, 16)
            for k, w in enumerate((w_q, w_k, w_v)):
                sp.dma_start(w_raw[:, k, :], w).then_inc(ld_raw, 16)
            for half in range(2):
                sp.dma_start(u_raw[HD * half:HD * (half + 1), :, :],
                             w_u.rearrange("(h d) e -> d h e", d=HD)).then_inc(ld_raw, 16)
            sp.dma_start(w2_all[:, :, :], w_2.rearrange("e (f p) n -> p (e f) n", p=P)).then_inc(ld_w2, 16)
            sp.dma_start(wr_sb[:, :], w_r).then_inc(ld_wr, 16)
            sp.dma_start(br_sb[:, :], b_r.rearrange("(a e) -> a e", a=1).to_broadcast([P, NX])).then_inc(ld_wr, 16)
            w_pairs = wsplit_dram.rearrange("g p (s n) -> p g s n", n=P)
            for k in range(3):
                sp.wait_ge(w_split, 2 * (k + 1))
                sp.dma_start(w_pairs[:, :, 2 * k:2 * k + 2, :], w_st[:, k % 2].bitcast(F32)).then_inc(w_saved[k], 16)
            for h in range(2):
                sp.wait_ge(w_split, 6 + 3 * (h + 1))
                sp.dma_start(w_pairs[:, :, WQKV + 2 * h:WQKV + 2 * h + 2, :],
                             w_st[:, (3 + h) % 2].bitcast(F32)).then_inc(w_saved[3 + h], 16)
            for saved in w_saved:
                sp.wait_ge(saved, 16)
            for k in range(2):
                sp.wait_ge(gT_sb, k + 1)
                sp.dma_start(gate_dram[P * k:P * (k + 1), :], gateT[:, k, :]).then_inc(gT_out, 16)
            sp.wait_ge(gT_out, 32)
            meet(sp, 1)

            def load_expert(e, parity):
                sp.dma_start(w_ffn[:, 0, :], w_1[e]).then_inc(ld_e, 16)
                sp.dma_start(w_ffn[:, 1, :].rearrange("p (f n) -> p f n", n=P),
                             w_2[e].rearrange("(f p) n -> p f n", p=P)).then_inc(ld_e, 16)
                sp.dma_start(par[parity][:, :], ptab[:, e, :]).then_inc(ld_e, 16)
                sp.dma_start(g_bc[parity][:, :], gate_rows[bass.ds(e, 1), :].to_broadcast([P, TOK])).then_inc(ld_e, 16)

            load_expert(0, 0)
            w_split_count, block_count = sp.alloc_register("w_split_count"), sp.alloc_register("block_count")
            sp.reg_mov(w_split_count, 2)
            sp.reg_mov(block_count, 0)
            with sp.Fori(0, NX // 2) as it:
                for half in range(2):
                    sp.wait_ge(phase, ENGINES)
                    sp.wait_ge(w_hi_done, w_split_count)
                    sp.wait_ge(w_lo_done, w_split_count)
                    sp.wait_ge(y_added, block_count)
                    load_expert((it * 2 + 1 + half) % NX, 1 - half)
                    sp.reg_add(w_split_count, w_split_count, 2)
                    sp.reg_add(block_count, block_count, NG)
            meet(sp, 2)
            meet(sp, 3)

            def load_qkv(pair):
                sp.dma_start(w_qkv[:, :, :].bitcast(F32),
                             wsplit_dram[bass.ds(pair, 1), :, 0:WQKV * P].rearrange("a p (s n) -> (a p) s n", n=P)
                             ).then_inc(ld_qkv, 16)

            def load_out(pair):
                sp.dma_start(w_out[:, :, :].bitcast(F32),
                             wsplit_dram[bass.ds(pair, 1), :, WQKV * P:WALL * P].rearrange(
                                 "a p (s n) -> (a p) s n", n=P)).then_inc(ld_out, 16)

            def spread_qk(h):
                src = slice(HD * h, HD * (h + 1))
                for dst, st in ((qq[h][0:HD], q_st[src, 0]), (qq[h][HD:P], q_st[src, 1]),
                                (kh[h][0:HD], k_st[src, 0]), (kh[h][HD:P], k_st[src, 0]),
                                (kl[h][0:HD], k_st[src, 1]), (kl[h][HD:P], k_st[src, 1])):
                    sp.dma_start(dst.bitcast(F32), st.bitcast(F32)).then_inc(qk_in[h], 16)

            def dup_o(h, g, k):
                sp.wait_ge(o_hi, k)
                sp.dma_start(o_2[HD:P, h, BLK * g:BLK * (g + 1)].bitcast(F32),
                             o_1[0:HD, h, BLK * g:BLK * (g + 1)].bitcast(F32)).then_inc(o_dup, 16)

            load_qkv(0)
            load_out(0)
            sp.wait_ge(aux_free, 4)
            spread_qk(0)
            spread_qk(1)
            sp.wait_ge(aux_ready, AUX0)
            load_qkv(1)
            with sp.Fori(0, STEPS) as it:
                this_pair, after_next = sp.snap(it % PAIRS), sp.snap((it + 2) % PAIRS)
                dup_o(1, 1, it * 4 + 1)
                dup_o(0, 0, it * 4 + 2)
                sp.wait_ge(aux_ready, it * AUX + AUX0 + Y1 + 1)
                load_out(this_pair)
                sp.wait_ge(aux_free, it * AUX + AUX0 + K1 + 1)
                sp.wait_ge(s_ready, it * SLOTS + TB)
                spread_qk(0)
                sp.wait_ge(aux_ready, it * AUX + AUX0 + V1 + 1)
                load_qkv(after_next)
                dup_o(0, 1, it * 4 + 3)
                sp.wait_ge(s_ready, it * SLOTS + 2 * TB)
                spread_qk(1)
                dup_o(1, 0, it * 4 + 4)
            dup_o(1, 1, STEPS * 4 + 1)
            sp.dma_start(res[:, :, :], x_t).then_inc(ld_res, 16)
            for g in range(NG):
                sp.wait_ge(f_done, g + 1)
                sp.dma_start(out_t[:, TG * g:TG * (g + 1), :], res[:, TG * g:TG * (g + 1), :]).then_inc(stored, 16)
            sp.wait_ge(stored, 16 * NG)
            sp.wait_ge(ld_qkv, 16 * (STEPS + 2))
            sp.wait_ge(ld_out, 16 * (STEPS + 1))
            for h in range(2):
                sp.wait_ge(qk_in[h], 96 * (STEPS + 1))

        @block.gpsimd
        def _(pool):
            nc.gpsimd.memset(rows[:, :], 0.0).then_inc(made, 1)
            nc.gpsimd.memset(ident[:, :], 0.0).then_inc(made, 1)
            nc.gpsimd.memset(ident_bf[:, :], 0.0).then_inc(made, 1)
            nc.gpsimd.memset(causal[:, :], 0.0).then_inc(made, 1)
            pool.wait_ge(made, 4)
            for m in (ident, ident_bf):
                nc.gpsimd.affine_select(out=m[:, :], in_=m[:, :], compare_op=ALU.not_equal, fill=1.0,
                                        base=0, pattern=[[-1, P]], channel_multiplier=1).then_inc(made, 1)
            nc.gpsimd.affine_select(out=causal[:, :], in_=causal[:, :], compare_op=ALU.is_ge, fill=MASKED,
                                    base=0, pattern=[[-1, P]], channel_multiplier=1).then_inc(made, 1)

            def scale_rows(t, norm):
                for c in range(NB):
                    v = t[:, TB * c:TB * (c + 1), :]
                    pool.wait_ge(rstd_done, norm * NB + c + 1)
                    r = stat[:, norm, 4, TB * c:TB * (c + 1)].unsqueeze(2).to_broadcast([P, TB, P])
                    nc.gpsimd.tensor_tensor(v, v, r, ALU.mult).then_inc(normed, 1)

            def split(k, dst, hi_src):
                src = w_raw[:, k, :].rearrange("p (g n) -> p g n", n=P)
                nc.gpsimd.tensor_scalar(dst[:, :, 0, :], src, 1.0, 1.0, ALU.mult, ALU.mult).then_inc(w_split, 1)
                pool.wait_ge(w_split, 2 * k + 1)
                nc.gpsimd.tensor_tensor(dst[:, :, 1, :], src, dst[:, :, 0, :].bitcast(F32),
                                        ALU.subtract).then_inc(w_split, 1)

            pool.wait_ge(ld_raw, 5 * 16)
            split(0, w_st[:, 0], None)
            split(1, w_st[:, 1], None)
            scale_rows(xs, 0)
            pool.wait_ge(w_saved[0], 16)
            split(2, w_st[:, 0], None)
            scale_rows(xs2, 1)
            for h in range(2):
                pool.wait_ge(w_saved[1 + h], 16)
                pool.wait_ge(w_split, 6 + 3 * h)
                dst = w_st[:, (3 + h) % 2]
                u = u_raw[:, h::2, :]
                nc.gpsimd.tensor_scalar(dst[:, :, 0, :], u, 1.0, 1.0, ALU.mult, ALU.mult).then_inc(w_split, 1)
                nc.gpsimd.tensor_scalar(dst[0:HD, :, 1, :], u[0:HD], 1.0, 1.0, ALU.mult, ALU.mult).then_inc(w_split, 1)
                pool.wait_ge(w_split, 6 + 3 * h + 2)
                nc.gpsimd.tensor_tensor(dst[HD:P, :, 1, :], u[HD:P], dst[HD:P, :, 0, :].bitcast(F32),
                                        ALU.subtract).then_inc(w_split, 1)
            pool.wait_ge(w_split, 12)
            for g in range(NG):
                pool.wait_ge(x2_f, g + 1)
                s = slice(BLK * g, BLK * (g + 1))
                nc.gpsimd.tensor_scalar(x2T_hi[:, s], x2T[:, s], 1.0, 1.0, ALU.mult, ALU.mult).then_inc(x2_hi, 1)
            meet(pool, 1)

            def counter(name, value):
                r = pool.alloc_register(name)
                pool.reg_mov(r, value)
                return r

            def wait_next(signal, count, by=1):
                pool.reg_add(count, count, by)
                pool.wait_ge(made, MADE)
                pool.wait_ge(signal, count)

            def split_hi(parity):
                wait_next(ld_e, loads, 64)
                nc.gpsimd.tensor_scalar(w1_hi[parity][:, :], w_ffn[:, 0, :], 1.0, 1.0, ALU.mult, ALU.mult
                                        ).then_inc(w_hi_done, 1)
                nc.gpsimd.tensor_scalar(w2_hi[parity][:, :], w_ffn[:, 1, :], 1.0, 1.0, ALU.mult, ALU.mult
                                        ).then_inc(w_hi_done, 1)

            def hidden_hi(place):
                for f in range(FB):
                    wait_next(h_relu, relus)
                    nc.gpsimd.tensor_scalar(hid_hi[:, place, f, :], hid[:, f, :], 1.0, 1.0, ALU.mult, ALU.mult
                                            ).then_inc(h_hi, 1)

            loads, relus, outs = counter("loads", 0), counter("relus", 0), counter("outs", 0)
            split_hi(0)
            hidden_hi(0)
            with pool.Fori(0, NX // 2):
                for u in range(2 * NG):
                    if u % NG == 3:
                        split_hi(1 - u // NG)
                    if u > 0:
                        wait_next(y_ready, outs)
                    else:
                        pool.wait_ge(made, MADE)
                        pool.wait_ge(y_ready, outs)
                    hidden_hi((u + 1) % 2)
                pool.reg_add(outs, outs, 1)
            meet(pool, 2)

            zeroed = [vv[:, :, :, :], o_1[:, :, :], o_2[:, :, :]]
            zeroed += [t[:, :, :] for t in (*pT_hi, *pT_lo)]
            for t in zeroed:
                nc.gpsimd.memset(t.bitcast(F32), 0.0)
            meet(pool, 3)

            def normalise(m, i):
                wait_next(rec_done, recips)
                v = prb[:, m % 4, 0:P * (i + 1)]
                nc.gpsimd.tensor_scalar(v, v, rinv[:, m % 4:m % 4 + 1], 1.0, ALU.mult, ALU.mult).then_inc(norm_done, 1)

            recips = counter("recips", 0)
            normalise(0, 0)
            normalise(1, 1)
            with pool.Fori(0, STEPS):
                for s in range(SLOTS):
                    normalise(s + 2, (s + 2) % TB)

        @block.scalar
        def _(act):
            def square(t, norm):
                for c in range(NB):
                    v = slice(TB * c, TB * (c + 1))
                    act.wait_ge(centred, norm * NB + c + 1)
                    nc.scalar.activation(sq[:, v, :], t[:, v, :], ACT.Square).then_inc(squared, 1)

            def deviation(norm):
                for c in range(NB):
                    v = slice(TB * c, TB * (c + 1))
                    act.wait_ge(sd_done, (2 * norm) * NB + 2 * c + 1)
                    nc.scalar.activation(stat[:, norm, 3, v], stat[:, norm, 2, v], ACT.Sqrt).then_inc(sd_done, 1)

            square(xs, 0)
            deviation(0)
            square(xs2, 1)
            act.wait_ge(rowsT_sb, 1)
            for g in range(NG):
                act.wait_ge(xT_ready, g + 1)
                s = slice(BLK * g, BLK * (g + 1))
                nc.scalar.activation(acc[:, s], ps[:, g % 2, :], ACT.Identity, bias=cols[:, bu_row:bu_row + 1]
                                     ).then_inc(xT_hi, 1)
                nc.scalar.activation(xnT_hi[:, s], ps[:, g % 2, :], ACT.Copy).then_inc(xT_hi, 1)
                if g == 1:
                    deviation(1)
            for g in range(NG):
                act.wait_ge(x2_ready, g + 1)
                nc.scalar.activation(x2T[:, BLK * g:BLK * (g + 1)], ps[:, 2 + g % 2, :], ACT.Identity,
                                     scale=cols[:, gamma_row:gamma_row + 1],
                                     bias=cols[:, beta_row:beta_row + 1]).then_inc(x2_f, 1)
            act.wait_ge(shifted, 1)
            nc.scalar.activation(prob[:, :, :], logit[:, :, :], ACT.Exp).then_inc(exped, 1)
            meet(act, 1)

            def relu(m, parity, loads, reads):
                act.wait_ge(ld_e, loads)
                for f in range(FB):
                    act.wait_ge(h_ready, m * FB + f + 1)
                    if reads is not None:
                        act.wait_ge(h_lo, reads + f + 1)
                    nc.scalar.activation(hid[:, f, :], ps[:, f, :], ACT.Relu, bias=par[parity][:, f:f + 1]
                                         ).then_inc(h_relu, 1)

            relu(0, 0, 64, None)
            with act.Fori(0, NX // 2) as it:
                for u in range(2 * NG):
                    relu(it * (2 * NG) + u + 1, (u + 1) // NG % 2, it * 128 + 64 * ((u + 1) // NG + 1),
                         it * (2 * NG * FB) + u * FB)
            meet(act, 2)
            meet(act, 3)

            def exponent(m, i, count):
                act.wait_ge(max_done, count)
                nc.scalar.activation(prob_view(m, i), score_view(m, i), ACT.Exp,
                                     bias=nmax[:, m % 4:m % 4 + 1],
                                     accum_out=rsum[:, m % 4:m % 4 + 1]).then_inc(exp_done, 1)

            def stage_hi(st, half, scale, ready):
                act.wait_ge(aux_ready, ready)
                nc.scalar.activation(st[:, 0, BLK * half:BLK * (half + 1)], ps[:, AUX_BANK, :], ACT.Copy,
                                     scale=scale).then_inc(aux_hi, 1)

            for k in range(4):
                stage_hi(q_st if k < 2 else k_st, k % 2, QK_SCALE if k < 2 else 1.0, k + 1)
            for m in range(AHEAD):
                exponent(m, m, m + 1)
            with act.Fori(0, STEPS) as it:
                for s in range(SLOTS):
                    i, il, g = s % TB, s % TG, s % TB // TG
                    for c, (j, nj) in enumerate(chunks(i)):
                        act.wait_ge(t_ready, it * CHUNKS + chunk_no(s) + c + 1)
                        nc.scalar.activation(
                            pT_hi[g][:, j:j + nj, P * il:P * (il + 1)],
                            ps[:, PT_BANK + (chunk_no(s) + c) % 2, 0:P * nj].rearrange("p (j q) -> p j q", q=P),
                            ACT.Copy).then_inc(t_hi, 1)
                    exponent(s + AHEAD, (s + AHEAD) % TB, it * SLOTS + s + AHEAD + 1)
                    if s in (Q0, Q1, K0, K1):
                        if s in (Q0, K0):
                            for h in range(2):
                                act.wait_ge(qk_in[h], it * 96 + 96)
                        stage_hi(q_st if s < K0 else k_st, s % 2, QK_SCALE if s < K0 else 1.0,
                                 it * AUX + AUX0 + s + 1)
                    if s in (VT0, VT1):
                        act.wait_ge(aux_ready, it * AUX + AUX0 + s + 1)
                        j = TG * (s - VT0)
                        nc.scalar.activation(
                            vv[:, j:j + TG, :, 0:HD],
                            ps[:, AUX_BANK, :].rearrange("p (j h d) -> p j h d", h=2, d=HD),
                            ACT.Copy).then_inc(aux_hi, 1)
                    if s in PV_AT:
                        h, g = PV_AT[s]
                        act.wait_ge(o_ready, it * 4 + PV_NO[s] + 1)
                        nc.scalar.activation(o_1[:, h, BLK * g:BLK * (g + 1)], ps[:, O_BANK, :], ACT.Copy
                                             ).then_inc(o_hi, 1)
            act.wait_ge(o_ready, STEPS * 4 + 1)
            nc.scalar.activation(o_1[:, 1, BLK:N], ps[:, O_BANK, :], ACT.Copy).then_inc(o_hi, 1)

        @block.vector
        def _(dve):
            steps = [0]

            def step(ins):
                steps[0] += 1
                ins.then_inc(dve_step, 1)
                dve.wait_ge(dve_step, steps[0])

            def centre(src, dst, norm):
                for c in range(NB):
                    v = slice(TB * c, TB * (c + 1))
                    if norm == 0:
                        dve.wait_ge(ld_x[c], 16)
                    else:
                        dve.wait_ge(normed, c + 1)
                    step(nc.vector.tensor_reduce(stat[:, norm, 0, v], src[:, v, :], AX.X, ALU.add))
                    step(nc.vector.tensor_scalar(stat[:, norm, 1, v], stat[:, norm, 0, v], 1.0 / E, None, ALU.mult))
                    nc.vector.tensor_tensor(dst[:, v, :], src[:, v, :],
                                            stat[:, norm, 1, v].unsqueeze(2).to_broadcast([P, TB, P]),
                                            ALU.subtract).then_inc(centred, 1)

            def variance(norm):
                for c in range(NB):
                    v = slice(TB * c, TB * (c + 1))
                    dve.wait_ge(squared, norm * NB + c + 1)
                    step(nc.vector.tensor_reduce(stat[:, norm, 0, v], sq[:, v, :], AX.X, ALU.add))
                    nc.vector.tensor_scalar(stat[:, norm, 2, v], stat[:, norm, 0, v], 1.0 / E, LN_EPS,
                                            ALU.mult, ALU.add).then_inc(sd_done, 1)
                    dve.wait_ge(sd_done, (2 * norm) * NB + 2 * c + 2)
                    nc.vector.reciprocal(stat[:, norm, 4, v], stat[:, norm, 3, v]).then_inc(rstd_done, 1)

            centre(xs, xs, 0)
            variance(0)
            centre(xs, xs2, 1)
            dve.wait_ge(rowsT, 1)
            nc.vector.tensor_copy(cols[:, :], ps[:, 5, 0:P]).then_inc(rowsT_sb, 1)
            dve.wait_ge(rowsT_sb, 1)
            nc.vector.tensor_scalar(relu_b1[:, :], cols[:, 0:NX * FB], 0.0, None, ALU.max).then_inc(b1_relu, 1)
            variance(1)
            for g in range(NG):
                dve.wait_ge(xT_hi, 2 * g + 2)
                s = slice(BLK * g, BLK * (g + 1))
                nc.vector.tensor_tensor(xnT_lo[:, s], ps[:, g % 2, :], xnT_hi[:, s].bitcast(F32),
                                        ALU.subtract).then_inc(xT_lo, 1)
            dve.wait_ge(corr, 1)
            step(nc.vector.tensor_tensor(c_all[:, :], ps[:, 6, 0:NX], cols[:, b2_row:gamma_row], ALU.add))
            step(nc.vector.tensor_reduce(c_sum[:, 0:1], c_all[:, :], AX.X, ALU.add))
            nc.vector.tensor_copy(ptab[:, :, 0:FB], cols[:, 0:NX * FB].rearrange("p (e f) -> p e f", f=FB))
            nc.vector.tensor_scalar(ptab[:, :, FB], ps[:, 6, 0:NX], c_sum[:, 0:1], -1.0, ALU.subtract, ALU.mult)
            for g in range(NG):
                dve.wait_ge(x2_hi, g + 1)
                s = slice(BLK * g, BLK * (g + 1))
                nc.vector.tensor_tensor(x2T_lo[:, s], x2T[:, s], x2T_hi[:, s].bitcast(F32),
                                        ALU.subtract).then_inc(x2_lo, 1)

            def over_experts(row):
                return r_stat[:, row, :].unsqueeze(2).to_broadcast([P, NT, NX])

            dve.wait_ge(ld_wr, 32)
            dve.wait_ge(routed, 1)
            step(nc.vector.tensor_tensor(logit[:, :, :], ps[:, 4, 0:NT * NX].rearrange("p (t e) -> p t e", e=NX),
                                         br_sb[:, :].unsqueeze(1).to_broadcast([P, NT, NX]), ALU.add))
            step(nc.vector.tensor_reduce(r_stat[:, 0, :], logit[:, :, :], AX.X, ALU.max))
            nc.vector.tensor_tensor(logit[:, :, :], logit[:, :, :], over_experts(0), ALU.subtract).then_inc(shifted, 1)
            step(nc.vector.memset(rank[:, :, :], 0.0))
            dve.wait_ge(exped, 1)
            step(nc.vector.tensor_reduce(r_stat[:, 1, :], prob[:, :, :], AX.X, ALU.add))
            step(nc.vector.reciprocal(r_stat[:, 2, :], r_stat[:, 1, :]))
            step(nc.vector.tensor_tensor(prob[:, :, :], prob[:, :, :], over_experts(2), ALU.mult))
            for e in range(NX):
                b = beats[:, e % 2]
                mine = prob[:, :, e:e + 1]
                nc.vector.memset(b[:, :, e:e + 1], 0.0)
                if e > 0:
                    nc.vector.tensor_tensor(b[:, :, 0:e], mine.to_broadcast([P, NT, e]), prob[:, :, 0:e], ALU.is_gt)
                last = nc.vector.memset(c_sum[:, 1:2], 0.0)
                if e < NX - 1:
                    last = nc.vector.tensor_tensor(b[:, :, e + 1:NX], mine.to_broadcast([P, NT, NX - 1 - e]),
                                                   prob[:, :, e + 1:NX], ALU.is_ge)
                step(last)
                step(nc.vector.tensor_tensor(rank[:, :, :], rank[:, :, :], b, ALU.add))
            nc.vector.scalar_tensor_tensor(out=gate[:, :, :].rearrange("p e t -> p t e"), in0=rank[:, :, :], scalar=2.0,
                                           in1=prob[:, :, :], op0=ALU.is_lt, op1=ALU.mult).then_inc(gated_up, 1)
            for k in range(2):
                dve.wait_ge(gT_ready, 2)
                nc.vector.tensor_copy(gateT[:, k, :], ps[:, 7, P * k:P * (k + 1)]).then_inc(gT_sb, 1)
            meet(dve, 1)

            def split_lo(parity, count):
                for w, (hi, lo) in enumerate(((w1_hi, w1_lo), (w2_hi, w2_lo))):
                    dve.wait_ge(w_hi_done, count + w + 1)
                    nc.vector.tensor_tensor(lo[parity][:, :], w_ffn[:, w, :], hi[parity][:, :].bitcast(F32),
                                            ALU.subtract).then_inc(w_lo_done, 1)

            def hidden_lo(m, place):
                for f in range(FB):
                    dve.wait_ge(h_hi, m * FB + f + 1)
                    nc.vector.tensor_tensor(hid_lo[:, place, f, :], hid[:, f, :],
                                            hid_hi[:, place, f, :].bitcast(F32), ALU.subtract).then_inc(h_lo, 1)

            split_lo(0, 0)
            hidden_lo(0, 0)
            with dve.Fori(0, NX // 2) as it:
                for u in range(2 * NG):
                    n = it * (2 * NG) + u
                    if u % NG == 3:
                        split_lo(1 - u // NG, it * 4 + 2 * (u // NG + 1))
                    hidden_lo(n + 1, (u + 1) % 2)
                    s = slice(BLK * (u % NG), BLK * (u % NG + 1))
                    dve.wait_ge(y_ready, n + 1)
                    dve.wait_ge(y_added, n)
                    nc.vector.scalar_tensor_tensor(out=gated[:, :], in0=ps[:, 4, :],
                                                   scalar=par[u // NG][:, FB:FB + 1], in1=g_bc[u // NG][:, s],
                                                   op0=ALU.add, op1=ALU.mult).then_inc(y_gated, 1)
                    dve.wait_ge(y_gated, n + 1)
                    nc.vector.tensor_tensor(acc[:, s], acc[:, s], gated[:, :], ALU.add).then_inc(y_added, 1)
            meet(dve, 2)
            meet(dve, 3)

            def row_max(m, i, count):
                dve.wait_ge(s_ready, count)
                nc.vector.tensor_reduce(nmax[:, m % 4:m % 4 + 1], score_view(m, i), AX.X if i < TG else AX.XY,
                                        ALU.max, negate=True).then_inc(max_done, 1)

            def row_recip(m, count):
                dve.wait_ge(exp_done, count)
                nc.vector.reciprocal(rinv[:, m % 4:m % 4 + 1], rsum[:, m % 4:m % 4 + 1]).then_inc(rec_done, 1)

            def stage_lo(st, half, scale, his):
                dve.wait_ge(aux_hi, his)
                s = slice(BLK * half, BLK * (half + 1))
                nc.vector.scalar_tensor_tensor(out=st[:, 1, s], in0=ps[:, AUX_BANK, :], scalar=scale,
                                               in1=st[:, 0, s].bitcast(F32), op0=ALU.mult, op1=ALU.subtract
                                               ).then_inc(aux_free, 1)

            def stage_v(half, ready):
                dve.wait_ge(aux_ready, ready)
                nc.vector.tensor_copy(v_st[:, BLK * half:BLK * (half + 1)], ps[:, AUX_BANK, :]).then_inc(aux_free, 1)

            def add_out(half, block, ready):
                dve.wait_ge(aux_ready, ready)
                v = acc[:, bass.ts(block, BLK)]
                nc.vector.tensor_tensor(v, ps[:, AUX_BANK, :], v, ALU.add).then_inc(aux_free, 1)

            HIS0, HIS = 4, 6
            his_of = {Q0: 1, Q1: 2, VT0: 3, VT1: 4, K0: 5, K1: 6}
            for k in range(4):
                stage_lo(q_st if k < 2 else k_st, k % 2, QK_SCALE if k < 2 else 1.0, k + 1)
            for k in range(2):
                stage_v(k, 5 + k)
            for m in range(AHEAD):
                row_max(m, m, m + 1)
            row_recip(0, 1)
            row_recip(1, 2)
            for k in range(2):
                nc.vector.memset(spare[:, k:k + 1], 0.0).then_inc(t_free, 1)
            with dve.Fori(0, STEPS) as it:
                for s in range(SLOTS):
                    i, il, g = s % TB, s % TG, s % TB // TG
                    row_max(s + AHEAD, (s + AHEAD) % TB, it * SLOTS + s + AHEAD + 1)
                    row_recip(s + 2, it * SLOTS + s + 3)
                    for c, (j, nj) in enumerate(chunks(i)):
                        dve.wait_ge(t_hi, it * CHUNKS + chunk_no(s) + c + 1)
                        d = (slice(None), slice(j, j + nj), slice(P * il, P * (il + 1)))
                        nc.vector.tensor_tensor(
                            pT_lo[g][d],
                            ps[:, PT_BANK + (chunk_no(s) + c) % 2, 0:P * nj].rearrange("p (j q) -> p j q", q=P),
                            pT_hi[g][d].bitcast(F32), ALU.subtract).then_inc(t_free, 1)
                    if s in (Q0, Q1, K0, K1):
                        stage_lo(q_st if s < K0 else k_st, s % 2, QK_SCALE if s < K0 else 1.0,
                                 it * HIS + HIS0 + his_of[s])
                    if s in (VT0, VT1):
                        dve.wait_ge(aux_hi, it * HIS + HIS0 + his_of[s])
                        j = TG * (s - VT0)
                        nc.vector.tensor_tensor(
                            vv[:, j:j + TG, :, HD:P],
                            ps[:, AUX_BANK, :].rearrange("p (j h d) -> p j h d", h=2, d=HD),
                            vv[:, j:j + TG, :, 0:HD].bitcast(F32), ALU.subtract).then_inc(aux_free, 1)
                    if s in (Y0, Y1):
                        add_out(s - Y0, (it + STEPS - 1) % STEPS // PAIRS * GB + (s - Y0), it * AUX + AUX0 + s + 1)
                    if s in (V0, V1):
                        stage_v(s - V0, it * AUX + AUX0 + s + 1)
                    if s in PV_AT:
                        h, g = PV_AT[s]
                        dve.wait_ge(o_hi, it * 4 + PV_NO[s] + 1)
                        q = slice(BLK * g, BLK * (g + 1))
                        nc.vector.tensor_tensor(o_2[0:HD, h, q], ps[0:HD, O_BANK, :], o_1[0:HD, h, q].bitcast(F32),
                                                ALU.subtract).then_inc(o_lo, 1)
            dve.wait_ge(o_hi, STEPS * 4 + 1)
            nc.vector.tensor_tensor(o_2[0:HD, 1, BLK:N], ps[0:HD, O_BANK, :], o_1[0:HD, 1, BLK:N].bitcast(F32),
                                    ALU.subtract).then_inc(o_lo, 1)
            for half in range(GB):
                add_out(half, (NB - 1) * GB + half, STEPS * AUX + AUX0 + half + 1)
            dve.wait_ge(ld_res, 16)
            for g in range(NG):
                dve.wait_ge(f_ready, g + 1)
                v = res[:, TG * g:TG * (g + 1), :]
                nc.vector.tensor_tensor(v, ps[:, g % 2, :].rearrange("p (t e) -> p t e", e=P), v, ALU.add
                                        ).then_inc(f_done, 1)

        @block.tensor
        def _(pe):
            pe.wait_ge(made, MADE)
            pe.wait_ge(ld_rows, 5 * 16)
            pe.transpose(ps[:, 5, 0:P], rows[:, :], ident[:, :]).then_inc(rowsT, 1)
            for g in range(NG):
                pe.wait_ge(normed, g // 2 + 1)
                if g >= 2:
                    pe.wait_ge(xT_lo, g - 1)
                for t in range(TG):
                    mm = pe.transpose(ps[:, g % 2, P * t:P * (t + 1)], xs[:, TG * g + t, :], ident[:, :])
                mm.then_inc(xT_ready, 1)
            pe.wait_ge(b1_relu, 1)
            pe.wait_ge(ld_w2, 16)
            for e in range(NX):
                for f in range(FB):
                    mm = pe.matmul(ps[:, 6, e:e + 1], w2_all[:, e * FB + f, :], relu_b1[:, e * FB + f:e * FB + f + 1],
                                   start=(f == 0), stop=(f == FB - 1))
            mm.then_inc(corr, 1)
            for g in range(NG):
                pe.wait_ge(normed, NB + g // 2 + 1)
                if g >= 2:
                    pe.wait_ge(x2_f, g - 1)
                for t in range(TG):
                    mm = pe.transpose(ps[:, 2 + g % 2, P * t:P * (t + 1)], xs2[:, TG * g + t, :], ident[:, :])
                mm.then_inc(x2_ready, 1)
            pe.wait_ge(ld_wr, 32)
            for t in range(NT):
                if t % TG == 0:
                    pe.wait_ge(x2_f, t // TG + 1)
                mm = pe.matmul(ps[:, 4, NX * t:NX * (t + 1)], x2T[:, P * t:P * (t + 1)], wr_sb[:, :],
                               start=True, stop=True)
            mm.then_inc(routed, 1)
            pe.wait_ge(gated_up, 1)
            for k in range(2):
                pe.transpose(ps[:, 7, P * k:P * (k + 1)],
                             gate[:, :, :].rearrange("p e t -> p (e t)")[:, P * k:P * (k + 1)],
                             ident[:, :]).then_inc(gT_ready, 1)
            meet(pe, 1)

            def three(dst, w_hi, w_lo, m_hi, m_lo, start, stop):
                pe.matmul(dst, w_hi, m_hi, start=start, stop=False)
                pe.matmul(dst, w_hi, m_lo, start=False, stop=False)
                return pe.matmul(dst, w_lo, m_hi, start=False, stop=stop)

            def hidden(b, parity, splits, relus):
                pe.wait_ge(w_lo_done, splits)
                s = slice(BLK * b, BLK * (b + 1))
                for f in range(FB):
                    if relus is not None:
                        pe.wait_ge(h_relu, relus + f + 1)
                    c = slice(P * f, P * (f + 1))
                    three(ps[:, f, :], w1_hi[parity][:, c], w1_lo[parity][:, c], x2T_hi[:, s], x2T_lo[:, s],
                          True, True).then_inc(h_ready, 1)

            hidden(0, 0, 2, None)
            with pe.Fori(0, NX // 2) as it:
                for u in range(2 * NG):
                    n = it * (2 * NG) + u
                    ahead = (u + 1) // NG
                    hidden((u + 1) % NG, ahead % 2, it * 4 + 2 * (ahead + 1), n * FB)
                    pe.wait_ge(y_gated, n)
                    for f in range(FB):
                        pe.wait_ge(h_lo, n * FB + f + 1)
                        c = slice(P * f, P * (f + 1))
                        mm = three(ps[:, 4, :], w2_hi[u // NG][:, c], w2_lo[u // NG][:, c],
                                   hid_hi[:, u % 2, f, :], hid_lo[:, u % 2, f, :], f == 0, f == FB - 1)
                    mm.then_inc(y_ready, 1)
            meet(pe, 2)
            meet(pe, 3)

            aux = ps[:, AUX_BANK, :]

            def project(slot, block):
                s = bass.ts(block, BLK)
                three(aux, w_qkv[:, 2 * slot, :], w_qkv[:, 2 * slot + 1, :], xnT_hi[:, s], xnT_lo[:, s],
                      True, True).then_inc(aux_ready, 1)

            def scores(m, i, h):
                b, n = 2 * (m % 2), P * (i + 1)
                qt = qq[h][:, P * i:P * (i + 1)]
                halves = [(b, 0, max(n, 2 * P))] if i < TG else [(b, 0, n // 2), (b + 1, n // 2, n // 2)]
                for bank, k0, nk in halves:
                    last = bank == halves[-1][0]
                    pe.matmul(ps[:, bank, 0:nk], qt, kh[h][:, k0:k0 + nk], start=True, stop=False)
                    pe.matmul(ps[:, bank, 0:nk], qt, kl[h][:, k0:k0 + nk], start=False, stop=not last)
                    if last:
                        d = n - k0
                        pe.matmul(ps[:, bank, d - P:d], ident_bf[:, :], causal[:, :], start=False, stop=True
                                  ).then_inc(s_ready, 1)

            def transposes(m, bank, j, nj):
                for k in range(nj):
                    mm = pe.transpose(ps[:, bank, P * k:P * (k + 1)], prb[:, m % 4, P * (j + k):P * (j + k + 1)],
                                      ident[:, :])
                mm.then_inc(t_ready, 1)

            def weighted(h, g):
                nj = TG * (g + 1)
                for j in range(nj):
                    q0 = P * min(max(j - TG * g, 0), TG - 2)
                    for part, p in enumerate((pT_hi[g], pT_lo[g])):
                        mm = pe.matmul(ps[:, O_BANK, q0:BLK], vv[:, j, h, :], p[:, j, q0:BLK],
                                       start=(j == 0 and part == 0), stop=(j == nj - 1 and part == 1))
                mm.then_inc(o_ready, 1)

            def project_out(half):
                q = slice(BLK * half, BLK * (half + 1))
                for h in range(2):
                    pe.matmul(aux, w_out[:, 2 * h, :], o_1[:, h, q], start=(h == 0), stop=False)
                    mm = pe.matmul(aux, w_out[:, 2 * h + 1, :], o_2[:, h, q], start=False, stop=(h == 1))
                mm.then_inc(aux_ready, 1)

            pe.wait_ge(ld_qkv, 16)
            for k in range(AUX0):
                pe.wait_ge(aux_free, k)
                project(k // 2, k % 2)
            pe.wait_ge(qk_in[0], 96)
            for m in range(AHEAD):
                if m == 2:
                    pe.wait_ge(exp_done, 1)
                scores(m, m, 0)
            with pe.Fori(0, STEPS) as it:
                next_b = (it + 1) % STEPS // PAIRS * GB
                for s in range(SLOTS):
                    m = s + AHEAD
                    if m % TB == 0:
                        pe.wait_ge(qk_in[m // TB % 2], it * 96 + 96 * (1 + m // SLOTS))
                    pe.wait_ge(exp_done, it * SLOTS + m - 1)
                    scores(m, m % TB, m // TB % 2)
                    pe.wait_ge(norm_done, it * SLOTS + s + 1)
                    for c, (j, nj) in enumerate(chunks(s % TB)):
                        no = chunk_no(s) + c
                        pe.wait_ge(t_free, it * CHUNKS + no + 1)
                        transposes(s, PT_BANK + no % 2, j, nj)
                    if s < AUX:
                        pe.wait_ge(aux_free, it * AUX + AUX0 + s)
                    if s in (Q0, Q1):
                        if s == Q0:
                            pe.wait_ge(ld_qkv, it * 16 + 32)
                        project(0, next_b + s - Q0)
                    if s in (K0, K1):
                        project(1, next_b + s - K0)
                    if s in (V0, V1):
                        project(2, next_b + s - V0)
                    if s in (VT0, VT1):
                        for k in range(TG):
                            j = TG * (s - VT0) + k
                            mm = pe.transpose(ps[:, AUX_BANK, P * k:P * (k + 1)], v_st[:, P * j:P * (j + 1)],
                                              ident[:, :])
                        mm.then_inc(aux_ready, 1)
                    if s in (Y0, Y1):
                        if s == Y0:
                            pe.wait_ge(ld_out, it * 16 + 16)
                            pe.wait_ge(o_dup, it * 64 + 16)
                            pe.wait_ge(o_lo, it * 4 + 1)
                        project_out(s - Y0)
                    if s in PV_AT:
                        h, g = PV_AT[s]
                        pe.wait_ge(o_lo, it * 4 + PV_NO[s])
                        done = chunk_no(TB * h + TG * (g + 1)) - (CHUNKS if s == 1 else 0)
                        pe.wait_ge(t_free, it * CHUNKS + done + 2)
                        if s == TB - 3:
                            pe.wait_ge(aux_free, it * AUX + AUX0 + VT1 + 1)
                        weighted(h, g)
            pe.wait_ge(o_lo, STEPS * 4)
            pe.wait_ge(t_free, STEPS * CHUNKS + 2)
            weighted(1, 1)
            pe.wait_ge(ld_out, STEPS * 16 + 16)
            pe.wait_ge(o_dup, STEPS * 64 + 16)
            pe.wait_ge(o_lo, STEPS * 4 + 1)
            for half in range(GB):
                pe.wait_ge(aux_free, STEPS * AUX + AUX0 + half)
                project_out(half)
            pe.wait_ge(exp_done, STEPS * SLOTS + AHEAD)
            pe.wait_ge(aux_free, STEPS * AUX + AUX0 + GB)
            for g in range(NG):
                if g >= 2:
                    pe.wait_ge(f_done, g - 1)
                for t in range(TG):
                    mm = pe.transpose(ps[:, g % 2, P * t:P * (t + 1)], acc[:, BLK * g + P * t:BLK * g + P * (t + 1)],
                                      ident[:, :])
                mm.then_inc(f_ready, 1)


_INS = ["L0_attn_x", "L0_attn_w_q", "L0_attn_w_k", "L0_attn_w_v", "L0_attn_w_u", "L0_attn_b_u",
        "L0_ffn_gamma", "L0_ffn_beta", "L0_ffn_Wr", "L0_ffn_br", "L0_ffn_W1", "L0_ffn_b1",
        "L0_ffn_W2", "L0_ffn_b2"]


def kernel(**inputs):
    import numpy as np
    import concourse.bacc as bacc
    from concourse.bass_utils import run_bass_kernel_spmd

    nc = bacc.Bacc("TRN2", target_bir_lowering=False, num_devices=1)
    arrays, args = {}, []
    for name in _INS:
        a = np.ascontiguousarray(inputs[name])
        arrays[f"in_{name}"] = a
        args.append(nc.dram_tensor(f"in_{name}", a.shape, mybir.dt.from_np(a.dtype), kind="ExternalInput").ap())
    shape = arrays["in_L0_attn_x"].shape
    args.append(nc.dram_tensor("out_0", shape, F32, kind="ExternalOutput").ap())
    build(nc, *args)
    r = run_bass_kernel_spmd(nc, [arrays], core_ids=[0])
    return r.results[0]["out_0"]
```

```python
from contextlib import ExitStack

import concourse.bass as bass
from concourse import mybir

F32 = mybir.dt.float32
F32R = mybir.dt.float32r
BF16 = mybir.dt.bfloat16
ALU = mybir.AluOpType
ACT = mybir.ActivationFunctionType
AX = mybir.AxisListType

P = 128
LN_EPS = 1e-5
MASKED = -3.0e38


def build(nc, x, w_q, w_k, w_v, w_u, b_u, gamma, beta, w_r, b_r, w_1, b_1, w_2, b_2, out):
    NB, N, E = x.shape
    HD = 64
    H = w_q.shape[1] // HD
    NX, _, F = w_1.shape
    TOK = NB * N
    NT = TOK // P
    TB = N // P
    BLK = 512
    NG = TOK // BLK
    GB = N // BLK
    TG = BLK // P
    FB = F // P
    PAIRS = H // 2
    STEPS = NB * PAIRS
    SLOTS = 2 * TB
    QK_SCALE = 1.0 / HD
    assert E == P and N == 2 * BLK and F == BLK and NX == 8 and H % 2 == 0

    x_t = x.rearrange("b n e -> (b n) e").rearrange("(t p) e -> p t e", p=P)
    out_t = out.rearrange("b n e -> (b n) e").rearrange("(t p) e -> p t e", p=P)

    gate_dram = nc.dram_tensor("gate_rows", (NX * NT, P), F32).ap()
    gate_rows = gate_dram.rearrange("(e t) p -> e (t p)", e=NX)
    WQKV, WALL = 6, 10
    wsplit_dram = nc.dram_tensor("split_weights", (PAIRS, P, WALL * P), F32).ap()

    with ExitStack() as ctx:
        def sem(name):
            return ctx.enter_context(nc.semaphore(name))

        def sb(scope, name, shape, dt=F32):
            return scope.enter_context(nc.sbuf_tensor(name, shape, dt))

        ident = sb(ctx, "ident", [P, P])
        ident_bf = sb(ctx, "ident_bf", [P, P], BF16)
        causal = sb(ctx, "causal", [P, P], BF16)
        xnT_hi = sb(ctx, "xnT_hi", [P, TOK], F32R)
        xnT_lo = sb(ctx, "xnT_lo", [P, TOK], F32R)
        acc = sb(ctx, "acc", [P, TOK])

        spare = sb(ctx, "spare", [P, 8])

        early = ExitStack()
        x2T_hi = sb(early, "x2T_hi", [P, TOK], F32R)
        x2T_lo = sb(early, "x2T_lo", [P, TOK], F32R)
        ptab = sb(early, "ptab", [P, NX, FB + 1])

        setup = ExitStack()
        xs = sb(setup, "xs", [P, NT, P])
        xs2 = sb(setup, "xs2", [P, NT, P])
        sq = sb(setup, "sq", [P, NT, P])
        x2T = sb(setup, "x2T", [P, TOK])
        w2_all = sb(setup, "w2_all", [P, NX * FB, P])
        w_raw = sb(setup, "w_raw", [P, 3, H * HD])
        u_raw = sb(setup, "u_raw", [P, H, P])
        w_st = sb(setup, "w_st", [P, 2, PAIRS, 2, P], F32R)
        rows = sb(setup, "rows", [P, P])
        cols = sb(setup, "cols", [P, P])
        relu_b1 = sb(setup, "relu_b1", [P, NX * FB])
        b2_row, gamma_row, beta_row, bu_row = NX * FB, NX * FB + NX, NX * FB + NX + 1, NX * FB + NX + 2
        wr_sb = sb(setup, "wr_sb", [P, NX])
        br_sb = sb(setup, "br_sb", [P, NX])
        c_sum = sb(setup, "c_sum", [P, 2])
        c_all = sb(setup, "c_all", [P, NX])
        stat = sb(setup, "stat", [P, 2, 5, NT])
        logit = sb(setup, "logit", [P, NT, NX])
        prob = sb(setup, "prob", [P, NT, NX])
        r_stat = sb(setup, "r_stat", [P, 3, NT])
        rank = sb(setup, "rank", [P, NT, NX])
        beats = sb(setup, "beats", [P, 2, NT, NX])
        gate = sb(setup, "gate", [P, NX, NT])
        gateT = sb(setup, "gateT", [P, 2, P])
        setup.close()

        ffn = ExitStack()
        w_ffn = sb(ffn, "w_ffn", [P, 2, F])
        w1_hi = [sb(ffn, f"w1_hi{i}", [P, F], F32R) for i in range(2)]
        w1_lo = [sb(ffn, f"w1_lo{i}", [P, F], F32R) for i in range(2)]
        w2_hi = [sb(ffn, f"w2_hi{i}", [P, F], F32R) for i in range(2)]
        w2_lo = [sb(ffn, f"w2_lo{i}", [P, F], F32R) for i in range(2)]
        par = [sb(ffn, f"par{i}", [P, FB + 1]) for i in range(2)]
        g_bc = [sb(ffn, f"g_bc{i}", [P, TOK]) for i in range(2)]
        hid = sb(ffn, "hid", [P, FB, BLK])
        hid_hi = sb(ffn, "hid_hi", [P, 2, FB, BLK], F32R)
        hid_lo = sb(ffn, "hid_lo", [P, 2, FB, BLK], F32R)
        gated = sb(ffn, "gated", [P, BLK])
        ffn.close()
        early.close()

        att = ExitStack()
        w_qkv = sb(att, "w_qkv", [P, WQKV, P], F32R)
        w_out = sb(att, "w_out", [P, WALL - WQKV, P], F32R)
        q_st = sb(att, "q_st", [P, 2, N], F32R)
        k_st = sb(att, "k_st", [P, 2, N], F32R)
        v_st = sb(att, "v_st", [P, N])
        qq = [sb(att, f"qq{h}", [P, N], F32R) for h in range(2)]
        kh = [sb(att, f"kh{h}", [P, N], F32R) for h in range(2)]
        kl = [sb(att, f"kl{h}", [P, N], F32R) for h in range(2)]
        vv = sb(att, "vv", [P, TB, 2, P], F32R)
        prb = sb(att, "prb", [P, 4, N])
        pT_hi = [sb(att, f"pT_hi{g}", [P, TG * (g + 1), BLK], F32R) for g in range(GB)]
        pT_lo = [sb(att, f"pT_lo{g}", [P, TG * (g + 1), BLK], F32R) for g in range(GB)]
        o_1 = sb(att, "o_1", [P, 2, N], F32R)
        o_2 = sb(att, "o_2", [P, 2, N], F32R)
        nmax = sb(att, "nmax", [P, 4])
        rsum = sb(att, "rsum", [P, 4])
        rinv = sb(att, "rinv", [P, 4])
        res = sb(att, "res", [P, NT, P])
        att.close()

        ps = ctx.enter_context(nc.psum_tensor("ps", [P, 8, BLK], F32))

        phase = sem("phase")
        made = sem("made")
        ld_x = [sem(f"ld_x{c}") for c in range(NB)]
        ld_rows, ld_w2, ld_wr, ld_raw = sem("ld_rows"), sem("ld_w2"), sem("ld_wr"), sem("ld_raw")
        centred, squared, sd_done, rstd_done, normed = (
            sem("centred"), sem("squared"), sem("sd_done"), sem("rstd_done"), sem("normed"))
        dve_step = sem("dve_step")
        rowsT, rowsT_sb, b1_relu, corr = sem("rowsT"), sem("rowsT_sb"), sem("b1_relu"), sem("corr")
        xT_ready, xT_hi, xT_lo = sem("xT_ready"), sem("xT_hi"), sem("xT_lo")
        x2_ready, x2_f, x2_hi, x2_lo = sem("x2_ready"), sem("x2_f"), sem("x2_hi"), sem("x2_lo")
        routed, shifted, exped, gated_up, gT_ready, gT_sb, gT_out = (
            sem("routed"), sem("shifted"), sem("exped"), sem("gated_up"), sem("gT_ready"), sem("gT_sb"), sem("gT_out"))
        w_split, w_saved = sem("w_split"), [sem(f"w_saved{k}") for k in range(5)]
        ld_e, w_hi_done, w_lo_done = sem("ld_e"), sem("w_hi_done"), sem("w_lo_done")
        h_ready, h_relu, h_hi, h_lo = sem("h_ready"), sem("h_relu"), sem("h_hi"), sem("h_lo")
        y_ready, y_gated, y_added = sem("y_ready"), sem("y_gated"), sem("y_added")
        ld_qkv, ld_out = sem("ld_qkv"), sem("ld_out")
        aux_ready, aux_hi, aux_free = sem("aux_ready"), sem("aux_hi"), sem("aux_free")
        qk_in = [sem("qk_in_a"), sem("qk_in_b")]
        s_ready, max_done, exp_done, rec_done, norm_done = (
            sem("s_ready"), sem("max_done"), sem("exp_done"), sem("rec_done"), sem("norm_done"))
        t_ready, t_hi, t_free = sem("t_ready"), sem("t_hi"), sem("t_free")
        o_ready, o_hi, o_lo, o_dup = sem("o_ready"), sem("o_hi"), sem("o_lo"), [sem(f"o_dup{g}") for g in range(GB)]
        zeroed = sem("zeroed")
        ld_res, f_ready, f_done, stored = sem("ld_res"), sem("f_ready"), sem("f_done"), sem("stored")

        ENGINES = 5
        MADE = 7

        def meet(eng, k):
            eng.drain().then_inc(phase, 1)
            eng.wait_ge(phase, ENGINES * k)

        def chunks(i):
            return [(j, min(TG, i + 1 - j)) for j in range(0, i + 1, TG)]

        HEAD_CHUNKS = sum(len(chunks(i)) for i in range(TB))
        CHUNKS = 2 * HEAD_CHUNKS

        def chunk_no(s):
            return HEAD_CHUNKS * (s // TB) + sum(len(chunks(i)) for i in range(s % TB))

        AUX0 = 6
        AUX_AT = {0: "Q0", 1: "Y0", 2: "Q1", 3: "VT0", 4: "K0", 5: "K1", 6: "VT1", 7: "Y1", 10: "V0", 12: "V1"}
        AUX = len(AUX_AT)
        AUX_NO = {job: k for k, job in enumerate(AUX_AT.values())}
        PV_AT = {0: (1, 1, 0, 3), 1: (1, 1, 3, 5), 2: (1, 1, 5, 8),
                 TG: (0, 0, 0, 2), TG + 1: (0, 0, 2, 4),
                 TB: (0, 1, 0, 3), TB + 1: (0, 1, 3, 5), TB + 2: (0, 1, 5, 8),
                 TB + TG: (1, 0, 0, 2), TB + TG + 1: (1, 0, 2, 4)}
        EVAC_AT = {s + 1: (h, g) for s, (h, g, _, end) in PV_AT.items() if end == TG * (g + 1)}
        PV_NO = {(1, 1): 0, (0, 0): 1, (0, 1): 2, (1, 0): 3}
        PT_BANK, O_BANK, AUX_BANK = 4, 6, 7
        ZEROED = 7
        AHEAD = 4
        EXP_AHEAD = 3

        def score_view(m, i):
            b = 2 * (m % 2)
            if i < TG:
                return ps[:, b, 0:P * (i + 1)]
            return ps[:, b:b + 2, 0:P * (i + 1) // 2]

        def prob_view(m, i):
            v = prb[:, m % 4, 0:P * (i + 1)]
            return v if i < TG else v.rearrange("p (a n) -> p a n", a=2)

        block = ctx.enter_context(nc.Block())

        @block.sync
        def _(sp):
            for c in range(NB):
                sp.dma_start(xs[:, TB * c:TB * (c + 1), :], x_t[:, TB * c:TB * (c + 1), :]).then_inc(ld_x[c], 16)
            sp.wait_ge(made, 1)
            sp.dma_start(rows[0:b2_row, :], b_1.rearrange("e (f p) -> (e f) p", p=P)).then_inc(ld_rows, 16)
            sp.dma_start(rows[b2_row:gamma_row, :], b_2).then_inc(ld_rows, 16)
            sp.dma_start(rows[gamma_row:gamma_row + 1, :], gamma.rearrange("(a e) -> a e", a=1)).then_inc(ld_rows, 16)
            sp.dma_start(rows[beta_row:beta_row + 1, :], beta.rearrange("(a e) -> a e", a=1)).then_inc(ld_rows, 16)
            sp.dma_start(rows[bu_row:bu_row + 1, :], b_u.rearrange("(a e) -> a e", a=1)).then_inc(ld_rows, 16)
            for k, w in enumerate((w_q, w_k, w_v)):
                sp.dma_start(w_raw[:, k, :], w).then_inc(ld_raw, 16)
            for half in range(2):
                sp.dma_start(u_raw[HD * half:HD * (half + 1), :, :],
                             w_u.rearrange("(h d) e -> d h e", d=HD)).then_inc(ld_raw, 16)
            sp.dma_start(w2_all[:, :, :], w_2.rearrange("e (f p) n -> p (e f) n", p=P)).then_inc(ld_w2, 16)
            sp.dma_start(wr_sb[:, :], w_r).then_inc(ld_wr, 16)
            sp.dma_start(br_sb[:, :], b_r.rearrange("(a e) -> a e", a=1).to_broadcast([P, NX])).then_inc(ld_wr, 16)
            w_pairs = wsplit_dram.rearrange("g p (s n) -> p g s n", n=P)
            for k in range(3):
                sp.wait_ge(w_split, 2 * (k + 1))
                sp.dma_start(w_pairs[:, :, 2 * k:2 * k + 2, :], w_st[:, k % 2].bitcast(F32)).then_inc(w_saved[k], 16)
            for h in range(2):
                sp.wait_ge(w_split, 6 + 3 * (h + 1))
                sp.dma_start(w_pairs[:, :, WQKV + 2 * h:WQKV + 2 * h + 2, :],
                             w_st[:, (3 + h) % 2].bitcast(F32)).then_inc(w_saved[3 + h], 16)
            for saved in w_saved:
                sp.wait_ge(saved, 16)
            for k in range(2):
                sp.wait_ge(gT_sb, k + 1)
                sp.dma_start(gate_dram[P * k:P * (k + 1), :], gateT[:, k, :]).then_inc(gT_out, 16)
            sp.wait_ge(gT_out, 32)
            meet(sp, 1)

            def load_expert(e, parity):
                sp.dma_start(w_ffn[:, 0, :], w_1[e]).then_inc(ld_e, 16)
                sp.dma_start(w_ffn[:, 1, :].rearrange("p (f n) -> p f n", n=P),
                             w_2[e].rearrange("(f p) n -> p f n", p=P)).then_inc(ld_e, 16)
                sp.dma_start(par[parity][:, :], ptab[:, e, :]).then_inc(ld_e, 16)
                sp.dma_start(g_bc[parity][:, :], gate_rows[bass.ds(e, 1), :].to_broadcast([P, TOK])).then_inc(ld_e, 16)

            load_expert(0, 0)
            w_split_count, block_count = sp.alloc_register("w_split_count"), sp.alloc_register("block_count")
            sp.reg_mov(w_split_count, 2)
            sp.reg_mov(block_count, 1)
            with sp.Fori(0, NX // 2) as it:
                for half in range(2):
                    sp.wait_ge(phase, ENGINES)
                    sp.wait_ge(w_hi_done, w_split_count)
                    sp.wait_ge(w_lo_done, w_split_count)
                    sp.wait_ge(y_added, block_count)
                    load_expert((it * 2 + 1 + half) % NX, 1 - half)
                    sp.reg_add(w_split_count, w_split_count, 2)
                    sp.reg_add(block_count, block_count, NG)
            meet(sp, 2)

            def load_qkv(pair):
                sp.dma_start(w_qkv[:, :, :].bitcast(F32),
                             wsplit_dram[bass.ds(pair, 1), :, 0:WQKV * P].rearrange("a p (s n) -> (a p) s n", n=P)
                             ).then_inc(ld_qkv, 16)

            def load_out(pair):
                sp.dma_start(w_out[:, :, :].bitcast(F32),
                             wsplit_dram[bass.ds(pair, 1), :, WQKV * P:WALL * P].rearrange(
                                 "a p (s n) -> (a p) s n", n=P)).then_inc(ld_out, 16)

            def spread_qk(h):
                src = slice(HD * h, HD * (h + 1))
                for dst, st in ((qq[h][0:HD], q_st[src, 0]), (qq[h][HD:P], q_st[src, 1]),
                                (kh[h][0:HD], k_st[src, 0]), (kh[h][HD:P], k_st[src, 0]),
                                (kl[h][0:HD], k_st[src, 1]), (kl[h][HD:P], k_st[src, 1])):
                    sp.dma_start(dst.bitcast(F32), st.bitcast(F32)).then_inc(qk_in[h], 16)

            def dup_o(h, g, k):
                sp.wait_ge(o_hi, k)
                sp.dma_start(o_2[HD:P, h, BLK * g:BLK * (g + 1)].bitcast(F32),
                             o_1[0:HD, h, BLK * g:BLK * (g + 1)].bitcast(F32)).then_inc(o_dup[g], 16)

            load_qkv(0)
            load_out(0)
            sp.wait_ge(aux_free, 4)
            spread_qk(0)
            spread_qk(1)
            sp.wait_ge(aux_ready, AUX0)
            load_qkv(1)
            sp.wait_ge(zeroed, ZEROED)
            dup_o(1, 0, 1)
            with sp.Fori(0, STEPS) as it:
                this_pair, after_next = sp.snap(it % PAIRS), sp.snap((it + 2) % PAIRS)
                dup_o(1, 1, it * 4 + 2)
                sp.wait_ge(aux_free, it * AUX + AUX0 + AUX_NO["K1"] + 1)
                sp.wait_ge(s_ready, it * SLOTS + TB)
                spread_qk(0)
                dup_o(0, 0, it * 4 + 3)
                sp.wait_ge(aux_ready, it * AUX + AUX0 + AUX_NO["Y1"] + 1)
                load_out(this_pair)
                sp.wait_ge(s_ready, it * SLOTS + 2 * TB)
                spread_qk(1)
                dup_o(0, 1, it * 4 + 4)
                sp.wait_ge(aux_ready, it * AUX + AUX0 + AUX_NO["V1"] + 1)
                load_qkv(after_next)
                dup_o(1, 0, it * 4 + 5)
            dup_o(1, 1, STEPS * 4 + 2)
            sp.dma_start(res[:, :, :], x_t).then_inc(ld_res, 16)
            for g in range(NG):
                sp.wait_ge(f_done, g + 1)
                sp.dma_start(out_t[:, TG * g:TG * (g + 1), :], res[:, TG * g:TG * (g + 1), :]).then_inc(stored, 16)
            sp.wait_ge(stored, 16 * NG)
            sp.wait_ge(ld_qkv, 16 * (STEPS + 2))
            sp.wait_ge(ld_out, 16 * (STEPS + 1))
            for h in range(2):
                sp.wait_ge(qk_in[h], 96 * (STEPS + 1))

        @block.gpsimd
        def _(pool):
            nc.gpsimd.memset(rows[:, :], 0.0).then_inc(made, 1)
            nc.gpsimd.memset(ident[:, :], 0.0).then_inc(made, 1)
            nc.gpsimd.memset(ident_bf[:, :], 0.0).then_inc(made, 1)
            nc.gpsimd.memset(causal[:, :], 0.0).then_inc(made, 1)
            pool.wait_ge(made, 4)
            for m in (ident, ident_bf):
                nc.gpsimd.affine_select(out=m[:, :], in_=m[:, :], compare_op=ALU.not_equal, fill=1.0,
                                        base=0, pattern=[[-1, P]], channel_multiplier=1).then_inc(made, 1)
            nc.gpsimd.affine_select(out=causal[:, :], in_=causal[:, :], compare_op=ALU.is_ge, fill=MASKED,
                                    base=0, pattern=[[-1, P]], channel_multiplier=1).then_inc(made, 1)

            def scale_rows(t, norm):
                for c in range(NB):
                    v = t[:, TB * c:TB * (c + 1), :]
                    pool.wait_ge(rstd_done, norm * NB + c + 1)
                    r = stat[:, norm, 4, TB * c:TB * (c + 1)].unsqueeze(2).to_broadcast([P, TB, P])
                    nc.gpsimd.tensor_tensor(v, v, r, ALU.mult).then_inc(normed, 1)

            def split(k, dst, hi_src):
                src = w_raw[:, k, :].rearrange("p (g n) -> p g n", n=P)
                nc.gpsimd.tensor_scalar(dst[:, :, 0, :], src, 1.0, 1.0, ALU.mult, ALU.mult).then_inc(w_split, 1)
                pool.wait_ge(w_split, 2 * k + 1)
                nc.gpsimd.tensor_tensor(dst[:, :, 1, :], src, dst[:, :, 0, :].bitcast(F32),
                                        ALU.subtract).then_inc(w_split, 1)

            pool.wait_ge(ld_raw, 5 * 16)
            split(0, w_st[:, 0], None)
            split(1, w_st[:, 1], None)
            scale_rows(xs, 0)
            pool.wait_ge(w_saved[0], 16)
            split(2, w_st[:, 0], None)
            scale_rows(xs2, 1)
            for h in range(2):
                pool.wait_ge(w_saved[1 + h], 16)
                pool.wait_ge(w_split, 6 + 3 * h)
                dst = w_st[:, (3 + h) % 2]
                u = u_raw[:, h::2, :]
                nc.gpsimd.tensor_scalar(dst[:, :, 0, :], u, 1.0, 1.0, ALU.mult, ALU.mult).then_inc(w_split, 1)
                nc.gpsimd.tensor_scalar(dst[0:HD, :, 1, :], u[0:HD], 1.0, 1.0, ALU.mult, ALU.mult).then_inc(w_split, 1)
                pool.wait_ge(w_split, 6 + 3 * h + 2)
                nc.gpsimd.tensor_tensor(dst[HD:P, :, 1, :], u[HD:P], dst[HD:P, :, 0, :].bitcast(F32),
                                        ALU.subtract).then_inc(w_split, 1)
            pool.wait_ge(w_split, 12)
            for g in range(NG):
                pool.wait_ge(x2_f, g + 1)
                s = slice(BLK * g, BLK * (g + 1))
                nc.gpsimd.tensor_scalar(x2T_hi[:, s], x2T[:, s], 1.0, 1.0, ALU.mult, ALU.mult).then_inc(x2_hi, 1)
            meet(pool, 1)

            def counter(name, value):
                r = pool.alloc_register(name)
                pool.reg_mov(r, value)
                return r

            def wait_next(signal, count, by=1):
                pool.reg_add(count, count, by)
                pool.wait_ge(made, MADE)
                pool.wait_ge(signal, count)

            def split_hi(parity):
                wait_next(ld_e, loads, 64)
                nc.gpsimd.tensor_scalar(w1_hi[parity][:, :], w_ffn[:, 0, :], 1.0, 1.0, ALU.mult, ALU.mult
                                        ).then_inc(w_hi_done, 1)
                nc.gpsimd.tensor_scalar(w2_hi[parity][:, :], w_ffn[:, 1, :], 1.0, 1.0, ALU.mult, ALU.mult
                                        ).then_inc(w_hi_done, 1)

            def hidden_hi(place):
                for f in range(FB):
                    wait_next(h_relu, relus)
                    nc.gpsimd.tensor_scalar(hid_hi[:, place, f, :], hid[:, f, :], 1.0, 1.0, ALU.mult, ALU.mult
                                            ).then_inc(h_hi, 1)

            loads, relus, outs = counter("loads", 0), counter("relus", 0), counter("outs", 0)
            split_hi(0)
            hidden_hi(0)
            pool.reg_mov(outs, 1)
            with pool.Fori(0, NX // 2):
                for u in range(2 * NG):
                    if u % NG == 3:
                        split_hi(1 - u // NG)
                    pool.wait_ge(made, MADE)
                    pool.wait_ge(y_ready, outs)
                    pool.reg_add(outs, outs, 1)
                    hidden_hi((u + 1) % 2)
            meet(pool, 2)

            for t in (o_1[:, :, :], o_2[:, :, :], vv[:, :, :, :], pT_hi[1][:, :, :]):
                nc.gpsimd.memset(t.bitcast(F32), 0.0).then_inc(zeroed, 1)
            for t in (pT_hi[0], pT_lo[0]):
                nc.gpsimd.memset(t[:, TG - 1, P * (TG - 2):P * (TG - 1)].bitcast(F32), 0.0).then_inc(zeroed, 1)

            def normalise(m, i):
                wait_next(rec_done, recips)
                v = prb[:, m % 4, 0:P * (i + 1)]
                nc.gpsimd.tensor_scalar(v, v, rinv[:, m % 4:m % 4 + 1], 1.0, ALU.mult, ALU.mult).then_inc(norm_done, 1)

            recips = counter("recips", 0)
            normalise(0, 0)
            normalise(1, 1)
            with pool.Fori(0, STEPS):
                for s in range(SLOTS):
                    normalise(s + 2, (s + 2) % TB)

        @block.scalar
        def _(act):
            def square(t, norm):
                for c in range(NB):
                    v = slice(TB * c, TB * (c + 1))
                    act.wait_ge(centred, norm * NB + c + 1)
                    nc.scalar.activation(sq[:, v, :], t[:, v, :], ACT.Square).then_inc(squared, 1)

            def deviation(norm):
                for c in range(NB):
                    v = slice(TB * c, TB * (c + 1))
                    act.wait_ge(sd_done, (2 * norm) * NB + 2 * c + 1)
                    nc.scalar.activation(stat[:, norm, 3, v], stat[:, norm, 2, v], ACT.Sqrt).then_inc(sd_done, 1)

            square(xs, 0)
            deviation(0)
            square(xs2, 1)
            act.wait_ge(rowsT_sb, 1)
            for g in range(NG):
                act.wait_ge(xT_ready, g + 1)
                s = slice(BLK * g, BLK * (g + 1))
                nc.scalar.activation(acc[:, s], ps[:, g % 2, :], ACT.Identity, bias=cols[:, bu_row:bu_row + 1]
                                     ).then_inc(xT_hi, 1)
                nc.scalar.activation(xnT_hi[:, s], ps[:, g % 2, :], ACT.Copy).then_inc(xT_hi, 1)
                if g == 1:
                    deviation(1)
            for g in range(NG):
                act.wait_ge(x2_ready, g + 1)
                nc.scalar.activation(x2T[:, BLK * g:BLK * (g + 1)], ps[:, 2 + g % 2, :], ACT.Identity,
                                     scale=cols[:, gamma_row:gamma_row + 1],
                                     bias=cols[:, beta_row:beta_row + 1]).then_inc(x2_f, 1)
            act.wait_ge(shifted, 1)
            nc.scalar.activation(prob[:, :, :], logit[:, :, :], ACT.Exp).then_inc(exped, 1)
            meet(act, 1)

            def relu(m, parity, loads, reads):
                act.wait_ge(ld_e, loads)
                for f in range(FB):
                    act.wait_ge(h_ready, m * FB + f + 1)
                    if reads is not None:
                        act.wait_ge(h_lo, reads + f + 1)
                    nc.scalar.activation(hid[:, f, :], ps[:, f, :], ACT.Relu, bias=par[parity][:, f:f + 1]
                                         ).then_inc(h_relu, 1)

            relu(0, 0, 64, None)
            with act.Fori(0, NX // 2) as it:
                for u in range(2 * NG):
                    relu(it * (2 * NG) + u + 1, (u + 1) // NG % 2, it * 128 + 64 * ((u + 1) // NG + 1),
                         it * (2 * NG * FB) + u * FB)
            meet(act, 2)

            def exponent(m, i, count):
                act.wait_ge(max_done, count)
                nc.scalar.activation(prob_view(m, i), score_view(m, i), ACT.Exp,
                                     bias=nmax[:, m % 4:m % 4 + 1],
                                     accum_out=rsum[:, m % 4:m % 4 + 1]).then_inc(exp_done, 1)

            def stage_hi(st, half, scale, ready):
                act.wait_ge(aux_ready, ready)
                nc.scalar.activation(st[:, 0, BLK * half:BLK * (half + 1)], ps[:, AUX_BANK, :], ACT.Copy,
                                     scale=scale).then_inc(aux_hi, 1)

            def stage_v(half, ready):
                act.wait_ge(aux_ready, ready)
                nc.scalar.activation(v_st[:, BLK * half:BLK * (half + 1)], ps[:, AUX_BANK, :], ACT.Copy
                                     ).then_inc(aux_free, 1)

            for k in range(4):
                stage_hi(q_st if k < 2 else k_st, k % 2, QK_SCALE if k < 2 else 1.0, k + 1)
            for k in range(2):
                stage_v(k, 5 + k)
            for m in range(EXP_AHEAD):
                exponent(m, m, m + 1)
            with act.Fori(0, STEPS) as it:
                for s in range(SLOTS):
                    i, il, g = s % TB, s % TG, s % TB // TG
                    for c, (j, nj) in enumerate(chunks(i)):
                        act.wait_ge(t_ready, it * CHUNKS + chunk_no(s) + c + 1)
                        nc.scalar.activation(
                            pT_hi[g][:, j:j + nj, P * il:P * (il + 1)],
                            ps[:, PT_BANK + (chunk_no(s) + c) % 2, 0:P * nj].rearrange("p (j q) -> p j q", q=P),
                            ACT.Copy).then_inc(t_hi, 1)
                    job = AUX_AT.get(s)
                    ready = it * AUX + AUX0 + AUX_NO.get(job, 0) + 1
                    if job in ("Q0", "Q1", "K0", "K1"):
                        if job == "Q0":
                            for h in range(2):
                                act.wait_ge(qk_in[h], it * 96 + 96)
                        stage_hi(q_st if job[0] == "Q" else k_st, int(job[1]), QK_SCALE if job[0] == "Q" else 1.0,
                                 ready)
                    if job in ("VT0", "VT1"):
                        act.wait_ge(aux_ready, ready)
                        j = TG * int(job[2])
                        nc.scalar.activation(
                            vv[:, j:j + TG, :, 0:HD],
                            ps[:, AUX_BANK, :].rearrange("p (j h d) -> p j h d", h=2, d=HD),
                            ACT.Copy).then_inc(aux_hi, 1)
                    if job in ("V0", "V1"):
                        stage_v(int(job[1]), ready)
                    if s in EVAC_AT:
                        h, g = EVAC_AT[s]
                        act.wait_ge(o_ready, it * 4 + PV_NO[h, g] + 1)
                        nc.scalar.activation(o_1[:, h, BLK * g:BLK * (g + 1)], ps[:, O_BANK, :], ACT.Copy
                                             ).then_inc(o_hi, 1)
                    exponent(s + EXP_AHEAD, (s + EXP_AHEAD) % TB, it * SLOTS + s + EXP_AHEAD + 1)
            act.wait_ge(o_ready, STEPS * 4 + 1)
            nc.scalar.activation(o_1[:, 1, BLK:N], ps[:, O_BANK, :], ACT.Copy).then_inc(o_hi, 1)

        @block.vector
        def _(dve):
            steps = [0]

            def step(ins):
                steps[0] += 1
                ins.then_inc(dve_step, 1)
                dve.wait_ge(dve_step, steps[0])

            def centre(src, dst, norm):
                for c in range(NB):
                    v = slice(TB * c, TB * (c + 1))
                    if norm == 0:
                        dve.wait_ge(ld_x[c], 16)
                    else:
                        dve.wait_ge(normed, c + 1)
                    step(nc.vector.tensor_reduce(stat[:, norm, 0, v], src[:, v, :], AX.X, ALU.add))
                    step(nc.vector.tensor_scalar(stat[:, norm, 1, v], stat[:, norm, 0, v], 1.0 / E, None, ALU.mult))
                    nc.vector.tensor_tensor(dst[:, v, :], src[:, v, :],
                                            stat[:, norm, 1, v].unsqueeze(2).to_broadcast([P, TB, P]),
                                            ALU.subtract).then_inc(centred, 1)

            def variance(norm):
                for c in range(NB):
                    v = slice(TB * c, TB * (c + 1))
                    dve.wait_ge(squared, norm * NB + c + 1)
                    step(nc.vector.tensor_reduce(stat[:, norm, 0, v], sq[:, v, :], AX.X, ALU.add))
                    nc.vector.tensor_scalar(stat[:, norm, 2, v], stat[:, norm, 0, v], 1.0 / E, LN_EPS,
                                            ALU.mult, ALU.add).then_inc(sd_done, 1)
                    dve.wait_ge(sd_done, (2 * norm) * NB + 2 * c + 2)
                    nc.vector.reciprocal(stat[:, norm, 4, v], stat[:, norm, 3, v]).then_inc(rstd_done, 1)

            centre(xs, xs, 0)
            variance(0)
            centre(xs, xs2, 1)
            dve.wait_ge(rowsT, 1)
            nc.vector.tensor_copy(cols[:, :], ps[:, 5, 0:P]).then_inc(rowsT_sb, 1)
            dve.wait_ge(rowsT_sb, 1)
            nc.vector.tensor_scalar(relu_b1[:, :], cols[:, 0:NX * FB], 0.0, None, ALU.max).then_inc(b1_relu, 1)
            variance(1)
            for g in range(NG):
                dve.wait_ge(xT_hi, 2 * g + 2)
                s = slice(BLK * g, BLK * (g + 1))
                nc.vector.tensor_tensor(xnT_lo[:, s], ps[:, g % 2, :], xnT_hi[:, s].bitcast(F32),
                                        ALU.subtract).then_inc(xT_lo, 1)
            dve.wait_ge(corr, 1)
            step(nc.vector.tensor_tensor(c_all[:, :], ps[:, 6, 0:NX], cols[:, b2_row:gamma_row], ALU.add))
            step(nc.vector.tensor_reduce(c_sum[:, 0:1], c_all[:, :], AX.X, ALU.add))
            nc.vector.tensor_copy(ptab[:, :, 0:FB], cols[:, 0:NX * FB].rearrange("p (e f) -> p e f", f=FB))
            nc.vector.tensor_scalar(ptab[:, :, FB], ps[:, 6, 0:NX], c_sum[:, 0:1], -1.0, ALU.subtract, ALU.mult)
            for g in range(NG):
                dve.wait_ge(x2_hi, g + 1)
                s = slice(BLK * g, BLK * (g + 1))
                nc.vector.tensor_tensor(x2T_lo[:, s], x2T[:, s], x2T_hi[:, s].bitcast(F32),
                                        ALU.subtract).then_inc(x2_lo, 1)

            def over_experts(row):
                return r_stat[:, row, :].unsqueeze(2).to_broadcast([P, NT, NX])

            dve.wait_ge(ld_wr, 32)
            dve.wait_ge(routed, 1)
            step(nc.vector.tensor_tensor(logit[:, :, :], ps[:, 4, 0:NT * NX].rearrange("p (t e) -> p t e", e=NX),
                                         br_sb[:, :].unsqueeze(1).to_broadcast([P, NT, NX]), ALU.add))
            step(nc.vector.tensor_reduce(r_stat[:, 0, :], logit[:, :, :], AX.X, ALU.max))
            nc.vector.tensor_tensor(logit[:, :, :], logit[:, :, :], over_experts(0), ALU.subtract).then_inc(shifted, 1)
            step(nc.vector.memset(rank[:, :, :], 0.0))
            dve.wait_ge(exped, 1)
            step(nc.vector.tensor_reduce(r_stat[:, 1, :], prob[:, :, :], AX.X, ALU.add))
            step(nc.vector.reciprocal(r_stat[:, 2, :], r_stat[:, 1, :]))
            step(nc.vector.tensor_tensor(prob[:, :, :], prob[:, :, :], over_experts(2), ALU.mult))
            for e in range(NX):
                b = beats[:, e % 2]
                mine = prob[:, :, e:e + 1]
                nc.vector.memset(b[:, :, e:e + 1], 0.0)
                if e > 0:
                    nc.vector.tensor_tensor(b[:, :, 0:e], mine.to_broadcast([P, NT, e]), prob[:, :, 0:e], ALU.is_gt)
                last = nc.vector.memset(c_sum[:, 1:2], 0.0)
                if e < NX - 1:
                    last = nc.vector.tensor_tensor(b[:, :, e + 1:NX], mine.to_broadcast([P, NT, NX - 1 - e]),
                                                   prob[:, :, e + 1:NX], ALU.is_ge)
                step(last)
                step(nc.vector.tensor_tensor(rank[:, :, :], rank[:, :, :], b, ALU.add))
            nc.vector.scalar_tensor_tensor(out=gate[:, :, :].rearrange("p e t -> p t e"), in0=rank[:, :, :], scalar=2.0,
                                           in1=prob[:, :, :], op0=ALU.is_lt, op1=ALU.mult).then_inc(gated_up, 1)
            for k in range(2):
                dve.wait_ge(gT_ready, 2)
                nc.vector.tensor_copy(gateT[:, k, :], ps[:, 7, P * k:P * (k + 1)]).then_inc(gT_sb, 1)
            meet(dve, 1)

            def split_lo(parity, count):
                for w, (hi, lo) in enumerate(((w1_hi, w1_lo), (w2_hi, w2_lo))):
                    dve.wait_ge(w_hi_done, count + w + 1)
                    nc.vector.tensor_tensor(lo[parity][:, :], w_ffn[:, w, :], hi[parity][:, :].bitcast(F32),
                                            ALU.subtract).then_inc(w_lo_done, 1)

            def hidden_lo(m, place):
                for f in range(FB):
                    dve.wait_ge(h_hi, m * FB + f + 1)
                    nc.vector.tensor_tensor(hid_lo[:, place, f, :], hid[:, f, :],
                                            hid_hi[:, place, f, :].bitcast(F32), ALU.subtract).then_inc(h_lo, 1)

            for k, free in enumerate((y_ready, y_gated, y_added)):
                nc.vector.memset(spare[:, k:k + 1], 0.0).then_inc(free, 1)
            split_lo(0, 0)
            hidden_lo(0, 0)
            with dve.Fori(0, NX // 2) as it:
                for u in range(2 * NG):
                    n = it * (2 * NG) + u
                    if u % NG == 3:
                        split_lo(1 - u // NG, it * 4 + 2 * (u // NG + 1))
                    hidden_lo(n + 1, (u + 1) % 2)
                    s = slice(BLK * (u % NG), BLK * (u % NG + 1))
                    dve.wait_ge(y_ready, n + 2)
                    dve.wait_ge(y_added, n + 1)
                    nc.vector.scalar_tensor_tensor(out=gated[:, :], in0=ps[:, 4, :],
                                                   scalar=par[u // NG][:, FB:FB + 1], in1=g_bc[u // NG][:, s],
                                                   op0=ALU.add, op1=ALU.mult).then_inc(y_gated, 1)
                    dve.wait_ge(y_gated, n + 2)
                    nc.vector.tensor_tensor(acc[:, s], acc[:, s], gated[:, :], ALU.add).then_inc(y_added, 1)
            meet(dve, 2)

            def row_max(m, i, count):
                dve.wait_ge(s_ready, count)
                nc.vector.tensor_reduce(nmax[:, m % 4:m % 4 + 1], score_view(m, i), AX.X if i < TG else AX.XY,
                                        ALU.max, negate=True).then_inc(max_done, 1)

            def row_recip(m, count):
                dve.wait_ge(exp_done, count)
                nc.vector.reciprocal(rinv[:, m % 4:m % 4 + 1], rsum[:, m % 4:m % 4 + 1]).then_inc(rec_done, 1)

            def stage_lo(st, half, scale, his):
                dve.wait_ge(aux_hi, his)
                s = slice(BLK * half, BLK * (half + 1))
                nc.vector.scalar_tensor_tensor(out=st[:, 1, s], in0=ps[:, AUX_BANK, :], scalar=scale,
                                               in1=st[:, 0, s].bitcast(F32), op0=ALU.mult, op1=ALU.subtract
                                               ).then_inc(aux_free, 1)

            def add_out(half, block, ready):
                dve.wait_ge(aux_ready, ready)
                v = acc[:, bass.ts(block, BLK)]
                nc.vector.tensor_tensor(v, ps[:, AUX_BANK, :], v, ALU.add).then_inc(aux_free, 1)

            def out_lo(h, g, his):
                dve.wait_ge(o_hi, his)
                q = slice(BLK * g, BLK * (g + 1))
                nc.vector.tensor_tensor(o_2[0:HD, h, q], ps[0:HD, O_BANK, :], o_1[0:HD, h, q].bitcast(F32),
                                        ALU.subtract).then_inc(o_lo, 1)

            HIS0, HIS = 4, 6
            his_no = {job: k for k, job in enumerate(j for j in AUX_AT.values() if j[0] in "QK" or j[:2] == "VT")}
            for k in range(4):
                stage_lo(q_st if k < 2 else k_st, k % 2, QK_SCALE if k < 2 else 1.0, k + 1)
            nc.vector.memset(pT_lo[1][:, :, :].bitcast(F32), 0.0).then_inc(zeroed, 1)
            for m in range(AHEAD):
                row_max(m, m, m + 1)
            row_recip(0, 1)
            row_recip(1, 2)
            for k, free in enumerate((t_free, t_free, o_hi, o_lo)):
                nc.vector.memset(spare[:, 3 + k:4 + k], 0.0).then_inc(free, 1)
            with dve.Fori(0, STEPS) as it:
                for s in range(SLOTS):
                    i, il, g = s % TB, s % TG, s % TB // TG
                    row_recip(s + 2, it * SLOTS + s + 3)
                    for c, (j, nj) in enumerate(chunks(i)):
                        dve.wait_ge(t_hi, it * CHUNKS + chunk_no(s) + c + 1)
                        d = (slice(None), slice(j, j + nj), slice(P * il, P * (il + 1)))
                        nc.vector.tensor_tensor(
                            pT_lo[g][d],
                            ps[:, PT_BANK + (chunk_no(s) + c) % 2, 0:P * nj].rearrange("p (j q) -> p j q", q=P),
                            pT_hi[g][d].bitcast(F32), ALU.subtract).then_inc(t_free, 1)
                    job = AUX_AT.get(s)
                    his = it * HIS + HIS0 + his_no.get(job, 0) + 1
                    if job in ("Q0", "Q1", "K0", "K1"):
                        stage_lo(q_st if job[0] == "Q" else k_st, int(job[1]), QK_SCALE if job[0] == "Q" else 1.0, his)
                    if job in ("VT0", "VT1"):
                        dve.wait_ge(aux_hi, his)
                        j = TG * int(job[2])
                        nc.vector.tensor_tensor(
                            vv[:, j:j + TG, :, HD:P],
                            ps[:, AUX_BANK, :].rearrange("p (j h d) -> p j h d", h=2, d=HD),
                            vv[:, j:j + TG, :, 0:HD].bitcast(F32), ALU.subtract).then_inc(aux_free, 1)
                    if job in ("Y0", "Y1"):
                        half = int(job[1])
                        add_out(half, (it + STEPS - 1) % STEPS // PAIRS * GB + half, it * AUX + AUX0 + AUX_NO[job] + 1)
                    if s in EVAC_AT:
                        h, g = EVAC_AT[s]
                        out_lo(h, g, it * 4 + PV_NO[h, g] + 2)
                    row_max(s + AHEAD, (s + AHEAD) % TB, it * SLOTS + s + AHEAD + 1)
            out_lo(1, 1, STEPS * 4 + 2)
            for half in range(GB):
                add_out(half, (NB - 1) * GB + half, STEPS * AUX + AUX0 + half + 1)
            dve.wait_ge(ld_res, 16)
            for g in range(NG):
                dve.wait_ge(f_ready, g + 1)
                v = res[:, TG * g:TG * (g + 1), :]
                nc.vector.tensor_tensor(v, ps[:, g % 2, :].rearrange("p (t e) -> p t e", e=P), v, ALU.add
                                        ).then_inc(f_done, 1)

        @block.tensor
        def _(pe):
            pe.wait_ge(made, MADE)
            pe.wait_ge(ld_rows, 5 * 16)
            pe.transpose(ps[:, 5, 0:P], rows[:, :], ident[:, :]).then_inc(rowsT, 1)
            for g in range(NG):
                pe.wait_ge(normed, g // 2 + 1)
                if g >= 2:
                    pe.wait_ge(xT_lo, g - 1)
                for t in range(TG):
                    mm = pe.transpose(ps[:, g % 2, P * t:P * (t + 1)], xs[:, TG * g + t, :], ident[:, :])
                mm.then_inc(xT_ready, 1)
            pe.wait_ge(b1_relu, 1)
            pe.wait_ge(ld_w2, 16)
            for e in range(NX):
                for f in range(FB):
                    mm = pe.matmul(ps[:, 6, e:e + 1], w2_all[:, e * FB + f, :], relu_b1[:, e * FB + f:e * FB + f + 1],
                                   start=(f == 0), stop=(f == FB - 1))
            mm.then_inc(corr, 1)
            for g in range(NG):
                pe.wait_ge(normed, NB + g // 2 + 1)
                if g >= 2:
                    pe.wait_ge(x2_f, g - 1)
                for t in range(TG):
                    mm = pe.transpose(ps[:, 2 + g % 2, P * t:P * (t + 1)], xs2[:, TG * g + t, :], ident[:, :])
                mm.then_inc(x2_ready, 1)
            pe.wait_ge(ld_wr, 32)
            for t in range(NT):
                if t % TG == 0:
                    pe.wait_ge(x2_f, t // TG + 1)
                mm = pe.matmul(ps[:, 4, NX * t:NX * (t + 1)], x2T[:, P * t:P * (t + 1)], wr_sb[:, :],
                               start=True, stop=True)
            mm.then_inc(routed, 1)
            pe.wait_ge(gated_up, 1)
            for k in range(2):
                pe.transpose(ps[:, 7, P * k:P * (k + 1)],
                             gate[:, :, :].rearrange("p e t -> p (e t)")[:, P * k:P * (k + 1)],
                             ident[:, :]).then_inc(gT_ready, 1)
            meet(pe, 1)

            def three(dst, w_hi, w_lo, m_hi, m_lo, start, stop):
                pe.matmul(dst, w_hi, m_hi, start=start, stop=False)
                pe.matmul(dst, w_hi, m_lo, start=False, stop=False)
                return pe.matmul(dst, w_lo, m_hi, start=False, stop=stop)

            def hidden(b, parity, splits, relus):
                pe.wait_ge(w_lo_done, splits)
                s = slice(BLK * b, BLK * (b + 1))
                for f in range(FB):
                    if relus is not None:
                        pe.wait_ge(h_relu, relus + f + 1)
                    c = slice(P * f, P * (f + 1))
                    three(ps[:, f, :], w1_hi[parity][:, c], w1_lo[parity][:, c], x2T_hi[:, s], x2T_lo[:, s],
                          True, True).then_inc(h_ready, 1)

            hidden(0, 0, 2, None)
            with pe.Fori(0, NX // 2) as it:
                for u in range(2 * NG):
                    n = it * (2 * NG) + u
                    ahead = (u + 1) // NG
                    hidden((u + 1) % NG, ahead % 2, it * 4 + 2 * (ahead + 1), n * FB)
                    pe.wait_ge(y_gated, n + 1)
                    for f in range(FB):
                        pe.wait_ge(h_lo, n * FB + f + 1)
                        c = slice(P * f, P * (f + 1))
                        mm = three(ps[:, 4, :], w2_hi[u // NG][:, c], w2_lo[u // NG][:, c],
                                   hid_hi[:, u % 2, f, :], hid_lo[:, u % 2, f, :], f == 0, f == FB - 1)
                    mm.then_inc(y_ready, 1)
            meet(pe, 2)

            aux = ps[:, AUX_BANK, :]

            def project(slot, block):
                s = bass.ts(block, BLK)
                three(aux, w_qkv[:, 2 * slot, :], w_qkv[:, 2 * slot + 1, :], xnT_hi[:, s], xnT_lo[:, s],
                      True, True).then_inc(aux_ready, 1)

            def scores(m, i, h):
                b, n = 2 * (m % 2), P * (i + 1)
                qt = qq[h][:, P * i:P * (i + 1)]
                halves = [(b, 0, max(n, 2 * P))] if i < TG else [(b, 0, n // 2), (b + 1, n // 2, n // 2)]
                for bank, k0, nk in halves:
                    last = bank == halves[-1][0]
                    pe.matmul(ps[:, bank, 0:nk], qt, kh[h][:, k0:k0 + nk], start=True, stop=False)
                    pe.matmul(ps[:, bank, 0:nk], qt, kl[h][:, k0:k0 + nk], start=False, stop=not last)
                    if last:
                        d = n - k0
                        pe.matmul(ps[:, bank, d - P:d], ident_bf[:, :], causal[:, :], start=False, stop=True
                                  ).then_inc(s_ready, 1)

            def transposes(m, bank, j, nj):
                for k in range(nj):
                    mm = pe.transpose(ps[:, bank, P * k:P * (k + 1)], prb[:, m % 4, P * (j + k):P * (j + k + 1)],
                                      ident[:, :])
                mm.then_inc(t_ready, 1)

            def weighted(h, g, first, end):
                for j in range(first, end):
                    q0 = P * min(max(j - TG * g, 0), TG - 2)
                    last = j == TG * (g + 1) - 1
                    for part, p in enumerate((pT_hi[g], pT_lo[g])):
                        mm = pe.matmul(ps[:, O_BANK, q0:BLK], vv[:, j, h, :], p[:, j, q0:BLK],
                                       start=(j == 0 and part == 0), stop=(last and part == 1))
                if last:
                    mm.then_inc(o_ready, 1)

            def project_out(half):
                q = slice(BLK * half, BLK * (half + 1))
                for h in range(2):
                    pe.matmul(aux, w_out[:, 2 * h, :], o_1[:, h, q], start=(h == 0), stop=False)
                    mm = pe.matmul(aux, w_out[:, 2 * h + 1, :], o_2[:, h, q], start=False, stop=(h == 1))
                mm.then_inc(aux_ready, 1)

            pe.wait_ge(ld_qkv, 16)
            for k in range(AUX0):
                pe.wait_ge(aux_free, k)
                project(k // 2, k % 2)
            pe.wait_ge(qk_in[0], 96)
            for m in range(AHEAD):
                if m >= 2:
                    pe.wait_ge(exp_done, m - 1)
                scores(m, m, 0)
            pe.wait_ge(zeroed, ZEROED)
            with pe.Fori(0, STEPS) as it:
                next_b = (it + 1) % STEPS // PAIRS * GB
                for s in range(SLOTS):
                    pe.wait_ge(norm_done, it * SLOTS + s + 1)
                    for c, (j, nj) in enumerate(chunks(s % TB)):
                        no = chunk_no(s) + c
                        pe.wait_ge(t_free, it * CHUNKS + no + 1)
                        transposes(s, PT_BANK + no % 2, j, nj)
                    job = AUX_AT.get(s)
                    if job:
                        pe.wait_ge(aux_free, it * AUX + AUX0 + AUX_NO[job])
                    if job in ("Q0", "Q1", "K0", "K1", "V0", "V1"):
                        if job == "Q0":
                            pe.wait_ge(ld_qkv, it * 16 + 32)
                        project("QKV".index(job[0]), next_b + int(job[1]))
                    if job in ("VT0", "VT1"):
                        for k in range(TG):
                            j = TG * int(job[2]) + k
                            mm = pe.transpose(ps[:, AUX_BANK, P * k:P * (k + 1)], v_st[:, P * j:P * (j + 1)],
                                              ident[:, :])
                        mm.then_inc(aux_ready, 1)
                    if job == "Y0":
                        pe.wait_ge(ld_out, it * 16 + 16)
                        pe.wait_ge(o_dup[0], it * 32 + 16)
                        pe.wait_ge(o_lo, it * 4 + 1)
                        project_out(0)
                    if job == "Y1":
                        pe.wait_ge(o_dup[1], it * 32 + 16)
                        pe.wait_ge(o_lo, it * 4 + 2)
                        project_out(1)
                    m = s + AHEAD
                    if m % TB == 0:
                        pe.wait_ge(qk_in[m // TB % 2], it * 96 + 96 * (1 + m // SLOTS))
                    pe.wait_ge(exp_done, it * SLOTS + m - 1)
                    scores(m, m % TB, m // TB % 2)
                    if s in PV_AT:
                        h, g, first, end = PV_AT[s]
                        if first == 0:
                            pe.wait_ge(o_lo, it * 4 + PV_NO[h, g] + 1)
                            done = chunk_no(TB * h + TG * (g + 1)) - (CHUNKS if s < TG else 0)
                            pe.wait_ge(t_free, it * CHUNKS + done + 2)
                        if (h, g, first) == (0, 0, 0):
                            pe.wait_ge(aux_free, it * AUX + AUX0 + AUX_NO["VT0"] + 1)
                        weighted(h, g, first, end)
            pe.wait_ge(o_lo, STEPS * 4 + 1)
            pe.wait_ge(t_free, STEPS * CHUNKS + 2)
            weighted(1, 1, 0, TB)
            pe.wait_ge(ld_out, STEPS * 16 + 16)
            for g in range(GB):
                pe.wait_ge(o_dup[g], STEPS * 32 + 16)
            pe.wait_ge(o_lo, STEPS * 4 + 2)
            for half in range(GB):
                pe.wait_ge(aux_free, STEPS * AUX + AUX0 + half)
                project_out(half)
            pe.wait_ge(exp_done, STEPS * SLOTS + EXP_AHEAD)
            pe.wait_ge(aux_free, STEPS * AUX + AUX0 + GB)
            for g in range(NG):
                if g >= 2:
                    pe.wait_ge(f_done, g - 1)
                for t in range(TG):
                    mm = pe.transpose(ps[:, g % 2, P * t:P * (t + 1)], acc[:, BLK * g + P * t:BLK * g + P * (t + 1)],
                                      ident[:, :])
                mm.then_inc(f_ready, 1)


_INS = ["L0_attn_x", "L0_attn_w_q", "L0_attn_w_k", "L0_attn_w_v", "L0_attn_w_u", "L0_attn_b_u",
        "L0_ffn_gamma", "L0_ffn_beta", "L0_ffn_Wr", "L0_ffn_br", "L0_ffn_W1", "L0_ffn_b1",
        "L0_ffn_W2", "L0_ffn_b2"]


def kernel(**inputs):
    import numpy as np
    import concourse.bacc as bacc
    from concourse.bass_utils import run_bass_kernel_spmd

    nc = bacc.Bacc("TRN2", target_bir_lowering=False, num_devices=1)
    arrays, args = {}, []
    for name in _INS:
        a = np.ascontiguousarray(inputs[name])
        arrays[f"in_{name}"] = a
        args.append(nc.dram_tensor(f"in_{name}", a.shape, mybir.dt.from_np(a.dtype), kind="ExternalInput").ap())
    shape = arrays["in_L0_attn_x"].shape
    args.append(nc.dram_tensor("out_0", shape, F32, kind="ExternalOutput").ap())
    build(nc, *args)
    r = run_bass_kernel_spmd(nc, [arrays], core_ids=[0])
    return r.results[0]["out_0"]
```

```python
from contextlib import ExitStack

import concourse.bass as bass
from concourse import mybir

F32 = mybir.dt.float32
F32R = mybir.dt.float32r
BF16 = mybir.dt.bfloat16
ALU = mybir.AluOpType
ACT = mybir.ActivationFunctionType
AX = mybir.AxisListType

P = 128
LN_EPS = 1e-5
MASKED = -3.0e38


def build(nc, x, w_q, w_k, w_v, w_u, b_u, gamma, beta, w_r, b_r, w_1, b_1, w_2, b_2, out):
    NB, N, E = x.shape
    HD = 64
    H = w_q.shape[1] // HD
    NX, _, F = w_1.shape
    TOK = NB * N
    NT = TOK // P
    TB = N // P
    BLK = 512
    NG = TOK // BLK
    GB = N // BLK
    TG = BLK // P
    FB = F // P
    PAIRS = H // 2
    STEPS = NB * PAIRS
    SLOTS = 2 * TB
    QK_SCALE = 1.0 / HD
    assert E == P and N == 2 * BLK and F == BLK and NX == 8 and H % 2 == 0

    x_t = x.rearrange("b n e -> (b n) e").rearrange("(t p) e -> p t e", p=P)
    out_t = out.rearrange("b n e -> (b n) e").rearrange("(t p) e -> p t e", p=P)

    gate_dram = nc.dram_tensor("gate_rows", (NX * NT, P), F32).ap()
    gate_rows = gate_dram.rearrange("(e t) p -> e (t p)", e=NX)
    WQKV, WALL = 6, 10
    wsplit_dram = nc.dram_tensor("split_weights", (PAIRS, P, WALL * P), F32).ap()

    with ExitStack() as ctx:
        def sem(name):
            return ctx.enter_context(nc.semaphore(name))

        def sb(scope, name, shape, dt=F32):
            return scope.enter_context(nc.sbuf_tensor(name, shape, dt))

        ident = sb(ctx, "ident", [P, P])
        ident_bf = sb(ctx, "ident_bf", [P, P], BF16)
        causal = sb(ctx, "causal", [P, P], BF16)
        xnT_hi = sb(ctx, "xnT_hi", [P, TOK], F32R)
        xnT_lo = sb(ctx, "xnT_lo", [P, TOK], F32R)
        acc = sb(ctx, "acc", [P, TOK])

        spare = sb(ctx, "spare", [P, 8])

        early = ExitStack()
        x2T_hi = sb(early, "x2T_hi", [P, TOK], F32R)
        x2T_lo = sb(early, "x2T_lo", [P, TOK], F32R)
        ptab = sb(early, "ptab", [P, NX, FB + 1])

        gateT = sb(early, "gateT", [P, 2, P])
        w_ffn = sb(early, "w_ffn", [P, 2, F])

        def expert_weights(scope, i):
            return [*(sb(scope, f"{w}{i}", [P, F], F32R) for w in ("w1_hi", "w1_lo", "w2_hi", "w2_lo")),
                    sb(scope, f"par{i}", [P, FB + 1])]

        even_expert = expert_weights(early, 0)

        setup = ExitStack()
        xs = sb(setup, "xs", [P, NT, P])
        sq = sb(setup, "sq", [P, NT, P])
        x2T = sb(setup, "x2T", [P, TOK])
        w2_all = sb(setup, "w2_all", [P, NX * FB, P])
        w_raw = sb(setup, "w_raw", [P, 3, H * HD])
        u_raw = sb(setup, "u_raw", [P, H, P])
        w_st = sb(setup, "w_st", [P, 2, PAIRS, 2, P], F32R)
        rows = sb(setup, "rows", [P, P])
        cols = sb(setup, "cols", [P, P])
        relu_b1 = sb(setup, "relu_b1", [P, NX * FB])
        b2_row, gamma_row, beta_row, bu_row = NX * FB, NX * FB + NX, NX * FB + NX + 1, NX * FB + NX + 2
        wr_sb = sb(setup, "wr_sb", [P, NX])
        br_sb = sb(setup, "br_sb", [P, NX])
        c_sum = sb(setup, "c_sum", [P, 2])
        c_all = sb(setup, "c_all", [P, NX])
        stat = sb(setup, "stat", [P, 2, 5, NT])
        var_1 = sb(setup, "var_1", [P, NT])
        logit = sb(setup, "logit", [P, NT, NX])
        prob = sb(setup, "prob", [P, NT, NX])
        r_stat = sb(setup, "r_stat", [P, 3, NT])
        rank = sb(setup, "rank", [P, NT, NX])
        beats = x2T[:, 0:NT * NX * NX].rearrange("p (t e f) -> p t e f", e=NX, f=NX)
        gate = sb(setup, "gate", [P, NX, NT])
        setup.close()

        ffn = ExitStack()
        w1_hi, w1_lo, w2_hi, w2_lo, par = zip(even_expert, expert_weights(ffn, 1))
        g_bc = [sb(ffn, f"g_bc{i}", [P, TOK]) for i in range(2)]
        hid = sb(ffn, "hid", [P, FB, BLK])
        hid_hi = sb(ffn, "hid_hi", [P, 2, FB, BLK], F32R)
        hid_lo = sb(ffn, "hid_lo", [P, 2, FB, BLK], F32R)
        gated = sb(ffn, "gated", [P, BLK])
        ffn.close()
        early.close()

        att = ExitStack()
        w_qkv = sb(att, "w_qkv", [P, WQKV, P], F32R)
        w_out = sb(att, "w_out", [P, WALL - WQKV, P], F32R)
        q_st = sb(att, "q_st", [P, 2, N], F32R)
        k_st = sb(att, "k_st", [P, 2, N], F32R)
        aux_f = sb(att, "aux_f", [P, 2, BLK])
        v_st = sb(att, "v_st", [P, N])
        qq = [sb(att, f"qq{h}", [P, N], F32R) for h in range(2)]
        kh = [sb(att, f"kh{h}", [P, N], F32R) for h in range(2)]
        kl = [sb(att, f"kl{h}", [P, N], F32R) for h in range(2)]
        vv = sb(att, "vv", [P, TB, 2, P], F32R)
        prb = sb(att, "prb", [P, 4, N])
        pT_hi = [sb(att, f"pT_hi{g}", [P, TG * (g + 1), BLK], F32R) for g in range(GB)]
        pT_lo = [sb(att, f"pT_lo{g}", [P, TG * (g + 1), BLK], F32R) for g in range(GB)]
        o_1 = sb(att, "o_1", [P, 2, N], F32R)
        o_2 = sb(att, "o_2", [P, 2, N], F32R)
        nmax = sb(att, "nmax", [P, 4])
        rsum = sb(att, "rsum", [P, 4])
        rinv = sb(att, "rinv", [P, 4])
        res = sb(att, "res", [P, NT, P])
        att.close()

        ps = ctx.enter_context(nc.psum_tensor("ps", [P, 8, BLK], F32))

        phase = sem("phase")
        made = sem("made")
        ld_x = [sem(f"ld_x{c}") for c in range(NB)]
        ld_rows, ld_w2, ld_wr, ld_raw = sem("ld_rows"), sem("ld_w2"), sem("ld_wr"), sem("ld_raw")
        centred, squared, sd_done, rstd_done, normed = (
            sem("centred"), sem("squared"), sem("sd_done"), sem("rstd_done"), sem("normed"))
        dve_step = sem("dve_step")
        rowsT, rowsT_sb, b1_relu, corr = sem("rowsT"), sem("rowsT_sb"), sem("b1_relu"), sem("corr")
        xT_ready, xT_hi, xT_lo = sem("xT_ready"), sem("xT_hi"), sem("xT_lo")
        x2_rows, x2_ready, x2_f, x2_hi, x2_lo = sem("x2_rows"), sem("x2_ready"), sem("x2_f"), sem("x2_hi"), sem("x2_lo")
        routed, shifted, exped, gated_up, gT_ready, gT_sb, gT_out = (
            sem("routed"), sem("shifted"), sem("exped"), sem("gated_up"), sem("gT_ready"), sem("gT_sb"), sem("gT_out"))
        w_split, w_saved = sem("w_split"), [sem(f"w_saved{k}") for k in range(5)]
        ld_e, ld_g, w_hi_done, w_lo_done = sem("ld_e"), [sem("ld_g_even"), sem("ld_g_odd")], sem("w_hi_done"), sem("w_lo_done")
        h_ready, h_relu, h_hi, h_lo = sem("h_ready"), sem("h_relu"), sem("h_hi"), sem("h_lo")
        y_ready, y_gated, y_added = sem("y_ready"), sem("y_gated"), sem("y_added")
        ld_qkv, ld_out = sem("ld_qkv"), sem("ld_out")
        aux_ready, aux_sb, aux_free = sem("aux_ready"), sem("aux_sb"), sem("aux_free")
        aux_hi, aux_lo = sem("aux_hi"), sem("aux_lo")
        qk_in = [sem("qk_in_a"), sem("qk_in_b")]
        s_ready, max_done, exp_done, rec_done, norm_done = (
            sem("s_ready"), sem("max_done"), sem("exp_done"), sem("rec_done"), sem("norm_done"))
        t_ready, t_hi, t_free = sem("t_ready"), sem("t_hi"), sem("t_free")
        o_ready, o_hi, o_lo, o_dup = sem("o_ready"), sem("o_hi"), sem("o_lo"), [sem(f"o_dup{g}") for g in range(GB)]
        zeroed = sem("zeroed")
        ld_res, f_ready, f_done, stored = sem("ld_res"), sem("f_ready"), sem("f_done"), sem("stored")

        ENGINES = 5
        EARLY_G = 4
        MADE = 8

        def meet(eng, k):
            eng.drain().then_inc(phase, 1)
            eng.wait_ge(phase, ENGINES * k)

        def chunks(i):
            if i < TG:
                return [(0, i + 1)]
            half = (i + 2) // 2
            return [(0, half), (half, i + 1 - half)]

        HEAD_CHUNKS = sum(len(chunks(i)) for i in range(TB))
        CHUNKS = 2 * HEAD_CHUNKS

        def chunk_no(s):
            return HEAD_CHUNKS * (s // TB) + sum(len(chunks(i)) for i in range(s % TB))

        AUX0 = 6
        AUX_AT = {0: "Q0", 1: "Y0", 2: "Q1", 3: "VT0", 4: "K0", 5: "Y1", 6: "VT1", 7: "K1", 10: "V0", 12: "V1"}
        AUX = len(AUX_AT)
        AUX_NO = {job: k for k, job in enumerate(AUX_AT.values())}
        SPLIT_NO = {job: k for k, job in enumerate(j for j in AUX_AT.values() if j[0] in "QK" or j[:2] == "VT")}
        SPLITS0, SPLITS = 4, len(SPLIT_NO)
        FREE_NO = {job: k for k, job in enumerate(j for j in AUX_AT.values() if j not in SPLIT_NO)}
        FREES0, FREES = AUX0 - SPLITS0, len(FREE_NO)
        PV_AT = {0: (1, 1, 0, 3), 1: (1, 1, 3, 5), 2: (1, 1, 5, 8),
                 TG + 1: (0, 0, 0, 2), TG + 2: (0, 0, 2, 4),
                 TB: (0, 1, 0, 3), TB + 1: (0, 1, 3, 5), TB + 2: (0, 1, 5, 8),
                 TB + TG: (1, 0, 0, 2), TB + TG + 1: (1, 0, 2, 4)}
        EVAC_AT = {s + 1: (h, g) for s, (h, g, _, end) in PV_AT.items() if end == TG * (g + 1)}
        PV_NO = {(1, 1): 0, (0, 0): 1, (0, 1): 2, (1, 0): 3}
        O_BANK = 6
        RING, SKIP_AFTER = (4, 5, 7), (9, 13)
        RING_BANK, RING_PLACES = {}, []
        for slot in range(SLOTS):
            items = [chunk_no(slot) + c for c in range(len(chunks(slot % TB)))]
            items += [AUX_AT[slot]] if slot in AUX_AT else []
            items += [None] if slot in SKIP_AFTER else []
            for item in items:
                RING_BANK[item] = RING[len(RING_PLACES) % len(RING)]
                RING_PLACES.append(item)
        assert len(RING_PLACES) % len(RING) == 0
        FREE0 = len(RING)

        def held_by(item):
            k = RING_PLACES.index(item) - len(RING)
            while RING_PLACES[k] is None:
                k -= len(RING)
            return RING_PLACES[k], k < 0
        ZEROED = 7
        AHEAD = 4
        EXP_AHEAD = 3

        SCORE_BANK = [*range(TG), *(2 * (i % 2) for i in range(TG, TB))]
        HELD_BY = [2, 3, 3, 4, 3, 2, 2, 2]

        def score_view(i):
            b = SCORE_BANK[i]
            if i < TG:
                return ps[:, b, 0:P * (i + 1)]
            return ps[:, b:b + 2, 0:P * (i + 1) // 2]

        def prob_view(m, i):
            v = prb[:, m % 4, 0:P * (i + 1)]
            return v if i < TG else v.rearrange("p (a n) -> p a n", a=2)

        def each_pair(eng):
            with eng.Fori(0, STEPS // 2) as turn:
                for u in range(2):
                    yield turn * 2 + u

        block = ctx.enter_context(nc.Block())

        @block.sync
        def _(sp):
            for c in range(NB):
                sp.dma_start(xs[:, TB * c:TB * (c + 1), :], x_t[:, TB * c:TB * (c + 1), :]).then_inc(ld_x[c], 16)
            sp.wait_ge(made, 1)
            sp.dma_start(rows[0:b2_row, :], b_1.rearrange("e (f p) -> (e f) p", p=P)).then_inc(ld_rows, 16)
            sp.dma_start(rows[b2_row:gamma_row, :], b_2).then_inc(ld_rows, 16)
            sp.dma_start(rows[gamma_row:gamma_row + 1, :], gamma.rearrange("(a e) -> a e", a=1)).then_inc(ld_rows, 16)
            sp.dma_start(rows[beta_row:beta_row + 1, :], beta.rearrange("(a e) -> a e", a=1)).then_inc(ld_rows, 16)
            sp.dma_start(rows[bu_row:bu_row + 1, :], b_u.rearrange("(a e) -> a e", a=1)).then_inc(ld_rows, 16)
            for k, w in enumerate((w_q, w_k, w_v)):
                sp.dma_start(w_raw[:, k, :], w).then_inc(ld_raw, 16)
            for half in range(2):
                sp.dma_start(u_raw[HD * half:HD * (half + 1), :, :],
                             w_u.rearrange("(h d) e -> d h e", d=HD)).then_inc(ld_raw, 16)
            sp.dma_start(w2_all[:, :, :], w_2.rearrange("e (f p) n -> p (e f) n", p=P)).then_inc(ld_w2, 16)
            sp.dma_start(wr_sb[:, :], w_r).then_inc(ld_wr, 16)
            sp.dma_start(br_sb[:, :], b_r.rearrange("(a e) -> a e", a=1).to_broadcast([P, NX])).then_inc(ld_wr, 16)

            def load_weights(e):
                sp.dma_start(w_ffn[:, 0, :], w_1[e]).then_inc(ld_e, 16)
                sp.dma_start(w_ffn[:, 1, :].rearrange("p (f n) -> p f n", n=P),
                             w_2[e].rearrange("(f p) n -> p f n", p=P)).then_inc(ld_e, 16)

            load_weights(0)
            w_pairs = wsplit_dram.rearrange("g p (s n) -> p g s n", n=P)
            for k in range(3):
                sp.wait_ge(w_split, 2 * (k + 1))
                sp.dma_start(w_pairs[:, :, 2 * k:2 * k + 2, :], w_st[:, k % 2].bitcast(F32)).then_inc(w_saved[k], 16)
            for h in range(2):
                sp.wait_ge(w_split, 6 + 3 * (h + 1))
                sp.dma_start(w_pairs[:, :, WQKV + 2 * h:WQKV + 2 * h + 2, :],
                             w_st[:, (3 + h) % 2].bitcast(F32)).then_inc(w_saved[3 + h], 16)
            for saved in w_saved:
                sp.wait_ge(saved, 16)
            for k in range(2):
                sp.wait_ge(gT_sb, k + 1)
                sp.dma_start(gate_dram[P * k:P * (k + 1), :], gateT[:, k, :]).then_inc(gT_out, 16)
            meet(sp, 1)

            def load_gates(e, parity):
                sp.dma_start(g_bc[parity][:, :], gate_rows[bass.ds(e, 1), :].to_broadcast([P, TOK])
                             ).then_inc(ld_g[parity], 16)

            sp.wait_ge(gT_out, 32)
            load_gates(0, 0)
            w_split_count, block_count = sp.alloc_register("w_split_count"), sp.alloc_register("block_count")
            sp.reg_mov(w_split_count, 2)
            sp.reg_mov(block_count, 1)
            with sp.Fori(0, NX // 2) as it:
                for half in range(2):
                    sp.wait_ge(phase, ENGINES)
                    sp.wait_ge(w_hi_done, w_split_count)
                    sp.wait_ge(w_lo_done, w_split_count)
                    sp.wait_ge(y_added, block_count)
                    e = (it * 2 + 1 + half) % NX
                    load_weights(e)
                    sp.dma_start(par[1 - half][:, :], ptab[:, e, :]).then_inc(ld_e, 16)
                    load_gates(e, 1 - half)
                    sp.reg_add(w_split_count, w_split_count, 2)
                    sp.reg_add(block_count, block_count, NG)
            meet(sp, 2)

            def load_qkv(pair):
                sp.dma_start(w_qkv[:, :, :].bitcast(F32),
                             wsplit_dram[bass.ds(pair, 1), :, 0:WQKV * P].rearrange("a p (s n) -> (a p) s n", n=P)
                             ).then_inc(ld_qkv, 16)

            def load_out(pair):
                sp.dma_start(w_out[:, :, :].bitcast(F32),
                             wsplit_dram[bass.ds(pair, 1), :, WQKV * P:WALL * P].rearrange(
                                 "a p (s n) -> (a p) s n", n=P)).then_inc(ld_out, 16)

            def spread_qk(h):
                src = slice(HD * h, HD * (h + 1))
                for dst, st in ((qq[h][0:HD], q_st[src, 0]), (qq[h][HD:P], q_st[src, 1]),
                                (kh[h][0:HD], k_st[src, 0]), (kh[h][HD:P], k_st[src, 0]),
                                (kl[h][0:HD], k_st[src, 1]), (kl[h][HD:P], k_st[src, 1])):
                    sp.dma_start(dst.bitcast(F32), st.bitcast(F32)).then_inc(qk_in[h], 16)

            def dup_o(h, g, k):
                sp.wait_ge(o_hi, k)
                sp.dma_start(o_2[HD:P, h, BLK * g:BLK * (g + 1)].bitcast(F32),
                             o_1[0:HD, h, BLK * g:BLK * (g + 1)].bitcast(F32)).then_inc(o_dup[g], 16)

            load_qkv(0)
            load_out(0)
            sp.wait_ge(aux_lo, SPLITS0)
            spread_qk(0)
            spread_qk(1)
            sp.wait_ge(aux_ready, AUX0)
            load_qkv(1)
            sp.wait_ge(zeroed, ZEROED)
            dup_o(1, 0, 1)
            for it in each_pair(sp):
                this_pair, after_next = sp.snap(it % PAIRS), sp.snap((it + 2) % PAIRS)
                dup_o(1, 1, it * 4 + 2)
                sp.wait_ge(aux_ready, it * AUX + AUX0 + AUX_NO["Y1"] + 1)
                load_out(this_pair)
                sp.wait_ge(aux_lo, it * SPLITS + SPLITS0 + SPLIT_NO["K1"] + 1)
                sp.wait_ge(s_ready, it * SLOTS + TB)
                spread_qk(0)
                dup_o(0, 0, it * 4 + 3)
                sp.wait_ge(s_ready, it * SLOTS + 2 * TB)
                spread_qk(1)
                dup_o(0, 1, it * 4 + 4)
                sp.wait_ge(aux_ready, it * AUX + AUX0 + AUX_NO["V1"] + 1)
                load_qkv(after_next)
                dup_o(1, 0, it * 4 + 5)
            dup_o(1, 1, STEPS * 4 + 2)
            sp.dma_start(res[:, :, :], x_t).then_inc(ld_res, 16)
            for g in range(NG):
                sp.wait_ge(f_done, g + 1)
                sp.dma_start(out_t[:, TG * g:TG * (g + 1), :], res[:, TG * g:TG * (g + 1), :]).then_inc(stored, 16)
            sp.wait_ge(stored, 16 * NG)
            sp.wait_ge(ld_qkv, 16 * (STEPS + 2))
            sp.wait_ge(ld_out, 16 * (STEPS + 1))
            for h in range(2):
                sp.wait_ge(qk_in[h], 96 * (STEPS + 1))

        @block.gpsimd
        def _(pool):
            nc.gpsimd.memset(rows[:, :], 0.0).then_inc(made, 1)
            nc.gpsimd.memset(ident[:, :], 0.0).then_inc(made, 1)
            nc.gpsimd.memset(ident_bf[:, :], 0.0).then_inc(made, 1)
            nc.gpsimd.memset(causal[:, :], 0.0).then_inc(made, 1)
            pool.wait_ge(made, 4)
            for m in (ident, ident_bf):
                nc.gpsimd.affine_select(out=m[:, :], in_=m[:, :], compare_op=ALU.not_equal, fill=1.0,
                                        base=0, pattern=[[-1, P]], channel_multiplier=1).then_inc(made, 1)
            nc.gpsimd.affine_select(out=causal[:, :], in_=causal[:, :], compare_op=ALU.is_ge, fill=MASKED,
                                    base=0, pattern=[[-1, P]], channel_multiplier=1).then_inc(made, 1)

            for c in range(NB):
                v = xs[:, TB * c:TB * (c + 1), :]
                pool.wait_ge(rstd_done, c + 1)
                r = stat[:, 0, 4, TB * c:TB * (c + 1)].unsqueeze(2).to_broadcast([P, TB, P])
                nc.gpsimd.tensor_tensor(v, v, r, ALU.mult).then_inc(normed, 1)
            for g in range(NG):
                pool.wait_ge(x2_f, g + 1)
                s = slice(BLK * g, BLK * (g + 1))
                nc.gpsimd.tensor_scalar(x2T_hi[:, s], x2T[:, s], 1.0, 1.0, ALU.mult, ALU.mult).then_inc(x2_hi, 1)

            def split_hi(parity):
                nc.gpsimd.tensor_scalar(w1_hi[parity][:, :], w_ffn[:, 0, :], 1.0, 1.0, ALU.mult, ALU.mult
                                        ).then_inc(w_hi_done, 1)
                nc.gpsimd.tensor_scalar(w2_hi[parity][:, :], w_ffn[:, 1, :], 1.0, 1.0, ALU.mult, ALU.mult
                                        ).then_inc(w_hi_done, 1)

            pool.wait_ge(ld_e, 32)
            split_hi(0)

            def split(k, dst):
                src = w_raw[:, k, :].rearrange("p (g n) -> p g n", n=P)
                nc.gpsimd.tensor_scalar(dst[:, :, 0, :], src, 1.0, 1.0, ALU.mult, ALU.mult).then_inc(w_split, 1)
                pool.wait_ge(w_split, 2 * k + 1)
                nc.gpsimd.tensor_tensor(dst[:, :, 1, :], src, dst[:, :, 0, :].bitcast(F32),
                                        ALU.subtract).then_inc(w_split, 1)

            pool.wait_ge(ld_raw, 5 * 16)
            nc.gpsimd.tensor_scalar(w_raw[:, 0, :], w_raw[:, 0, :], QK_SCALE, 1.0, ALU.mult, ALU.mult).then_inc(made, 1)
            pool.wait_ge(made, MADE)
            split(0, w_st[:, 0])
            split(1, w_st[:, 1])
            pool.wait_ge(w_saved[0], 16)
            split(2, w_st[:, 0])
            for h in range(2):
                pool.wait_ge(w_saved[1 + h], 16)
                pool.wait_ge(w_split, 6 + 3 * h)
                dst = w_st[:, (3 + h) % 2]
                u = u_raw[:, h::2, :]
                nc.gpsimd.tensor_scalar(dst[:, :, 0, :], u, 1.0, 1.0, ALU.mult, ALU.mult).then_inc(w_split, 1)
                nc.gpsimd.tensor_scalar(dst[0:HD, :, 1, :], u[0:HD], 1.0, 1.0, ALU.mult, ALU.mult).then_inc(w_split, 1)
                pool.wait_ge(w_split, 6 + 3 * h + 2)
                nc.gpsimd.tensor_tensor(dst[HD:P, :, 1, :], u[HD:P], dst[HD:P, :, 0, :].bitcast(F32),
                                        ALU.subtract).then_inc(w_split, 1)
            pool.wait_ge(w_split, 12)
            meet(pool, 1)

            def counter(name, value):
                r = pool.alloc_register(name)
                pool.reg_mov(r, value)
                return r

            def wait_next(signal, count, by=1):
                pool.reg_add(count, count, by)
                pool.wait_ge(made, MADE)
                pool.wait_ge(signal, count)

            def hidden_hi(place):
                for f in range(FB):
                    wait_next(h_relu, relus)
                    nc.gpsimd.tensor_scalar(hid_hi[:, place, f, :], hid[:, f, :], 1.0, 1.0, ALU.mult, ALU.mult
                                            ).then_inc(h_hi, 1)

            loads, relus, outs = counter("loads", 32), counter("relus", 0), counter("outs", 1)
            hidden_hi(0)
            with pool.Fori(0, NX // 2):
                for u in range(2 * NG):
                    if u % NG == 3:
                        wait_next(ld_e, loads, 48)
                        split_hi(1 - u // NG)
                    pool.wait_ge(made, MADE)
                    pool.wait_ge(y_ready, outs)
                    pool.reg_add(outs, outs, 1)
                    hidden_hi((u + 1) % 2)
            meet(pool, 2)

            def normalise(m, i):
                wait_next(rec_done, recips)
                v = prb[:, m % 4, 0:P * (i + 1)]
                nc.gpsimd.tensor_scalar(v, v, rinv[:, m % 4:m % 4 + 1], 1.0, ALU.mult, ALU.mult).then_inc(norm_done, 1)

            def split_aux(src, hi, lo):
                wait_next(aux_sb, staged)
                nc.gpsimd.tensor_scalar(hi, src, 1.0, 1.0, ALU.mult, ALU.mult).then_inc(aux_hi, 1)
                wait_next(aux_hi, his)
                nc.gpsimd.tensor_tensor(lo, src, hi.bitcast(F32), ALU.subtract).then_inc(aux_lo, 1)

            def split_qk(st, half, place):
                q = slice(BLK * half, BLK * (half + 1))
                split_aux(aux_f[:, place, :], st[:, 0, q], st[:, 1, q])

            recips, staged, his = counter("recips", 0), counter("staged", 0), counter("his", 0)
            spreads = counter("spreads", 0)
            for k in range(SPLITS0):
                split_qk(q_st if k < 2 else k_st, k % 2, k % 2)
            for t in (o_1[:, :, :], o_2[:, :, :], vv[:, :, :, :], pT_hi[1][:, :, :]):
                nc.gpsimd.memset(t.bitcast(F32), 0.0).then_inc(zeroed, 1)
            for t in (pT_hi[0], pT_lo[0]):
                nc.gpsimd.memset(t[:, TG - 1, P * (TG - 2):P * (TG - 1)].bitcast(F32), 0.0).then_inc(zeroed, 1)
            normalise(0, 0)
            normalise(1, 1)
            for it in each_pair(pool):
                for s in range(SLOTS):
                    normalise(s + 2, (s + 2) % TB)
                    job = AUX_AT.get(s)
                    if job == "Q0":
                        pool.reg_add(spreads, spreads, 96)
                        for h in range(2):
                            pool.wait_ge(made, MADE)
                            pool.wait_ge(qk_in[h], spreads)
                    if job in SPLIT_NO:
                        place = SPLIT_NO[job] % 2
                        if job[0] == "V":
                            j = TG * int(job[2])
                            split_aux(aux_f[:, place, :].rearrange("p (j h d) -> p j h d", h=2, d=HD),
                                      vv[:, j:j + TG, :, 0:HD], vv[:, j:j + TG, :, HD:P])
                        else:
                            split_qk(q_st if job[0] == "Q" else k_st, int(job[1]), place)

        @block.scalar
        def _(act):
            for c in range(NB):
                v = slice(TB * c, TB * (c + 1))
                if c == 2:
                    act.wait_ge(rowsT, 1)
                    nc.scalar.activation(cols[:, :], ps[:, 5, 0:P], ACT.Copy).then_inc(rowsT_sb, 1)
                    act.wait_ge(rowsT_sb, 1)
                    nc.scalar.activation(relu_b1[:, :], cols[:, 0:NX * FB], ACT.Relu).then_inc(b1_relu, 1)
                act.wait_ge(centred, c + 1)
                nc.scalar.activation(sq[:, v, :], xs[:, v, :], ACT.Square).then_inc(squared, 1)
            for c in range(NB):
                v = slice(TB * c, TB * (c + 1))
                act.wait_ge(sd_done, 2 * c + 1)
                nc.scalar.activation(stat[:, 0, 3, v], stat[:, 0, 2, v], ACT.Sqrt).then_inc(sd_done, 1)
            act.wait_ge(sd_done, 2 * NB + 1)
            nc.scalar.activation(stat[:, 1, 3, :], stat[:, 1, 2, :], ACT.Sqrt).then_inc(sd_done, 1)
            for g in range(NG):
                act.wait_ge(x2_ready, g + 1)
                nc.scalar.activation(x2T[:, BLK * g:BLK * (g + 1)], ps[:, 2 + g % 2, :], ACT.Identity,
                                     scale=cols[:, gamma_row:gamma_row + 1],
                                     bias=cols[:, beta_row:beta_row + 1]).then_inc(x2_f, 1)
            for g in range(NG):
                if g == EARLY_G:
                    act.wait_ge(shifted, 1)
                    nc.scalar.activation(prob[:, :, :], logit[:, :, :], ACT.Exp).then_inc(exped, 1)
                act.wait_ge(xT_ready, g + 1)
                s = slice(BLK * g, BLK * (g + 1))
                nc.scalar.activation(acc[:, s], ps[:, g % 2, :], ACT.Identity, bias=cols[:, bu_row:bu_row + 1]
                                     ).then_inc(xT_hi, 1)
                nc.scalar.activation(xnT_hi[:, s], ps[:, g % 2, :], ACT.Copy).then_inc(xT_hi, 1)
            meet(act, 1)

            def relu(m, parity, loads, reads):
                act.wait_ge(ld_e, loads)
                for f in range(FB):
                    act.wait_ge(h_ready, m * FB + f + 1)
                    if reads is not None:
                        act.wait_ge(h_lo, reads + f + 1)
                    nc.scalar.activation(hid[:, f, :], ps[:, f, :], ACT.Relu, bias=par[parity][:, f:f + 1]
                                         ).then_inc(h_relu, 1)

            relu(0, 0, 32, None)
            with act.Fori(0, NX // 2) as it:
                for u in range(2 * NG):
                    relu(it * (2 * NG) + u + 1, (u + 1) // NG % 2, it * 96 + 48 * ((u + 1) // NG) + 32,
                         it * (2 * NG * FB) + u * FB)
            meet(act, 2)

            def exponent(m, i, count):
                act.wait_ge(max_done, count)
                nc.scalar.activation(prob_view(m, i), score_view(i), ACT.Exp,
                                     bias=nmax[:, m % 4:m % 4 + 1],
                                     accum_out=rsum[:, m % 4:m % 4 + 1]).then_inc(exp_done, 1)

            def stage(bank, ready, los, place):
                act.wait_ge(aux_ready, ready)
                if los is not None:
                    act.wait_ge(aux_lo, los)
                nc.scalar.activation(aux_f[:, place, :], ps[:, bank, :], ACT.Copy).then_inc(aux_sb, 1)

            def stage_v(bank, half, ready):
                act.wait_ge(aux_ready, ready)
                nc.scalar.activation(v_st[:, BLK * half:BLK * (half + 1)], ps[:, bank, :], ACT.Copy
                                     ).then_inc(aux_free, 1)

            for k in range(4):
                stage(RING[k % 3], k + 1, k - 1 if k >= 2 else None, k % 2)
            for k in range(2):
                stage_v(RING[(4 + k) % 3], k, 5 + k)
            for m in range(EXP_AHEAD):
                exponent(m, m, m + 1)
            for it in each_pair(act):
                for s in range(SLOTS):
                    i, il, g = s % TB, s % TG, s % TB // TG
                    if s in EVAC_AT:
                        head, part = EVAC_AT[s]
                        act.wait_ge(o_ready, it * 4 + PV_NO[head, part] + 1)
                        nc.scalar.activation(o_1[:, head, BLK * part:BLK * (part + 1)], ps[:, O_BANK, :], ACT.Copy
                                             ).then_inc(o_hi, 1)
                    for c, (j, nj) in enumerate(chunks(i)):
                        act.wait_ge(t_ready, it * CHUNKS + chunk_no(s) + c + 1)
                        nc.scalar.activation(
                            pT_hi[g][:, j:j + nj, P * il:P * (il + 1)],
                            ps[:, RING_BANK[chunk_no(s) + c], 0:P * nj].rearrange("p (j q) -> p j q", q=P),
                            ACT.Copy).then_inc(t_hi, 1)
                    job = AUX_AT.get(s)
                    ready = it * AUX + AUX0 + AUX_NO.get(job, 0) + 1
                    if job in SPLIT_NO:
                        stage(RING_BANK[job], ready, it * SPLITS + SPLITS0 + SPLIT_NO[job] - 1, SPLIT_NO[job] % 2)
                    if job in ("V0", "V1"):
                        stage_v(RING_BANK[job], int(job[1]), ready)
                    exponent(s + EXP_AHEAD, (s + EXP_AHEAD) % TB, it * SLOTS + s + EXP_AHEAD + 1)
            act.wait_ge(o_ready, STEPS * 4 + 1)
            nc.scalar.activation(o_1[:, 1, BLK:N], ps[:, O_BANK, :], ACT.Copy).then_inc(o_hi, 1)

        @block.vector
        def _(dve):
            steps = [0]

            def step(ins):
                steps[0] += 1
                ins.then_inc(dve_step, 1)
                dve.wait_ge(dve_step, steps[0])

            for c in range(NB):
                v = slice(TB * c, TB * (c + 1))
                dve.wait_ge(ld_x[c], 16)
                step(nc.vector.tensor_reduce(stat[:, 0, 0, v], xs[:, v, :], AX.X, ALU.add))
                step(nc.vector.tensor_scalar(stat[:, 0, 1, v], stat[:, 0, 0, v], 1.0 / E, None, ALU.mult))
                nc.vector.tensor_tensor(xs[:, v, :], xs[:, v, :],
                                        stat[:, 0, 1, v].unsqueeze(2).to_broadcast([P, TB, P]),
                                        ALU.subtract).then_inc(centred, 1)
            for c in range(NB):
                v = slice(TB * c, TB * (c + 1))
                dve.wait_ge(squared, c + 1)
                step(nc.vector.tensor_reduce(stat[:, 0, 0, v], sq[:, v, :], AX.X, ALU.add))
                nc.vector.tensor_scalar(var_1[:, v], stat[:, 0, 0, v], 1.0 / E, None, ALU.mult)
                nc.vector.tensor_scalar(stat[:, 0, 2, v], stat[:, 0, 0, v], 1.0 / E, LN_EPS,
                                        ALU.mult, ALU.add).then_inc(sd_done, 1)
                dve.wait_ge(sd_done, 2 * c + 2)
                nc.vector.reciprocal(stat[:, 0, 4, v], stat[:, 0, 3, v]).then_inc(rstd_done, 1)
            dve.wait_ge(rstd_done, NB)
            step(nc.vector.tensor_tensor(stat[:, 1, 0, :], var_1[:, :], stat[:, 0, 4, :], ALU.mult))
            step(nc.vector.tensor_tensor(stat[:, 1, 1, :], stat[:, 1, 0, :], stat[:, 0, 4, :], ALU.mult))
            nc.vector.tensor_scalar(stat[:, 1, 2, :], stat[:, 1, 1, :], 1.0, LN_EPS, ALU.mult, ALU.add).then_inc(sd_done, 1)
            dve.wait_ge(sd_done, 2 * NB + 2)
            nc.vector.reciprocal(stat[:, 1, 4, :], stat[:, 1, 3, :]).then_inc(rstd_done, 1)
            dve.wait_ge(rstd_done, NB + 1)
            for c in range(NB):
                v = slice(TB * c, TB * (c + 1))
                dve.wait_ge(normed, c + 1)
                nc.vector.tensor_tensor(sq[:, v, :], xs[:, v, :],
                                        stat[:, 1, 4, v].unsqueeze(2).to_broadcast([P, TB, P]),
                                        ALU.mult).then_inc(x2_rows, 1)
            for g in range(NG):
                dve.wait_ge(x2_hi, g + 1)
                s = slice(BLK * g, BLK * (g + 1))
                nc.vector.tensor_tensor(x2T_lo[:, s], x2T[:, s], x2T_hi[:, s].bitcast(F32),
                                        ALU.subtract).then_inc(x2_lo, 1)

            def xn_lo(blocks):
                for g in blocks:
                    dve.wait_ge(xT_hi, 2 * g + 2)
                    s = slice(BLK * g, BLK * (g + 1))
                    nc.vector.tensor_tensor(xnT_lo[:, s], ps[:, g % 2, :], xnT_hi[:, s].bitcast(F32),
                                            ALU.subtract).then_inc(xT_lo, 1)

            def over_experts(row):
                return r_stat[:, row, :].unsqueeze(2).to_broadcast([P, NT, NX])

            dve.wait_ge(ld_wr, 32)
            dve.wait_ge(routed, 1)
            step(nc.vector.tensor_tensor(logit[:, :, :], ps[:, 4, 0:NT * NX].rearrange("p (t e) -> p t e", e=NX),
                                         br_sb[:, :].unsqueeze(1).to_broadcast([P, NT, NX]), ALU.add))
            step(nc.vector.tensor_reduce(r_stat[:, 0, :], logit[:, :, :], AX.X, ALU.max))
            nc.vector.tensor_tensor(logit[:, :, :], logit[:, :, :], over_experts(0), ALU.subtract).then_inc(shifted, 1)
            xn_lo(range(EARLY_G))
            dve.wait_ge(exped, 1)
            step(nc.vector.tensor_reduce(r_stat[:, 1, :], prob[:, :, :], AX.X, ALU.add))
            step(nc.vector.reciprocal(r_stat[:, 2, :], r_stat[:, 1, :]))
            step(nc.vector.tensor_tensor(prob[:, :, :], prob[:, :, :], over_experts(2), ALU.mult))
            for e in range(NX):
                mine = prob[:, :, e:e + 1]
                nc.vector.memset(beats[:, :, e, e], 0.0)
                if e > 0:
                    nc.vector.tensor_tensor(beats[:, :, 0:e, e], mine.to_broadcast([P, NT, e]), prob[:, :, 0:e], ALU.is_gt)
                if e < NX - 1:
                    nc.vector.tensor_tensor(beats[:, :, e + 1:NX, e], mine.to_broadcast([P, NT, NX - 1 - e]),
                                            prob[:, :, e + 1:NX], ALU.is_ge)
            step(nc.vector.memset(c_sum[:, 1:2], 0.0))
            step(nc.vector.tensor_reduce(rank[:, :, :], beats[:, :, :, :], AX.X, ALU.add))
            nc.vector.scalar_tensor_tensor(out=gate[:, :, :].rearrange("p e t -> p t e"), in0=rank[:, :, :], scalar=2.0,
                                           in1=prob[:, :, :], op0=ALU.is_lt, op1=ALU.mult).then_inc(gated_up, 1)
            dve.wait_ge(corr, 1)
            step(nc.vector.tensor_tensor(c_all[:, :], ps[:, 6, 0:NX], cols[:, b2_row:gamma_row], ALU.add))
            step(nc.vector.tensor_reduce(c_sum[:, 0:1], c_all[:, :], AX.X, ALU.add))
            nc.vector.tensor_copy(ptab[:, :, 0:FB], cols[:, 0:NX * FB].rearrange("p (e f) -> p e f", f=FB))
            step(nc.vector.tensor_scalar(ptab[:, :, FB], ps[:, 6, 0:NX], c_sum[:, 0:1], -1.0, ALU.subtract, ALU.mult))
            nc.vector.tensor_copy(par[0][:, :], ptab[:, 0, :])
            for k in range(2):
                dve.wait_ge(gT_ready, 2)
                nc.vector.tensor_copy(gateT[:, k, :], ps[:, 7, P * k:P * (k + 1)]).then_inc(gT_sb, 1)
            xn_lo(range(EARLY_G, NG))

            def split_lo(parity, count):
                for w, (hi, lo) in enumerate(((w1_hi, w1_lo), (w2_hi, w2_lo))):
                    dve.wait_ge(w_hi_done, count + w + 1)
                    nc.vector.tensor_tensor(lo[parity][:, :], w_ffn[:, w, :], hi[parity][:, :].bitcast(F32),
                                            ALU.subtract).then_inc(w_lo_done, 1)

            split_lo(0, 0)
            meet(dve, 1)

            def hidden_lo(m, place):
                for f in range(FB):
                    dve.wait_ge(h_hi, m * FB + f + 1)
                    nc.vector.tensor_tensor(hid_lo[:, place, f, :], hid[:, f, :],
                                            hid_hi[:, place, f, :].bitcast(F32), ALU.subtract).then_inc(h_lo, 1)

            for k, free in enumerate((y_ready, y_gated, y_added)):
                nc.vector.memset(spare[:, k:k + 1], 0.0).then_inc(free, 1)
            hidden_lo(0, 0)
            with dve.Fori(0, NX // 2) as it:
                for u in range(2 * NG):
                    n = it * (2 * NG) + u
                    if u % NG == 3:
                        split_lo(1 - u // NG, it * 4 + 2 * (u // NG + 1))
                    hidden_lo(n + 1, (u + 1) % 2)
                    s = slice(BLK * (u % NG), BLK * (u % NG + 1))
                    if u % NG == 0:
                        dve.wait_ge(ld_g[u // NG], it * 16 + 16)
                    dve.wait_ge(y_ready, n + 2)
                    dve.wait_ge(y_added, n + 1)
                    nc.vector.scalar_tensor_tensor(out=gated[:, :], in0=ps[:, 4, :],
                                                   scalar=par[u // NG][:, FB:FB + 1], in1=g_bc[u // NG][:, s],
                                                   op0=ALU.add, op1=ALU.mult).then_inc(y_gated, 1)
                    dve.wait_ge(y_gated, n + 2)
                    nc.vector.tensor_tensor(acc[:, s], acc[:, s], gated[:, :], ALU.add).then_inc(y_added, 1)
            dve.wait_ge(ld_g[0], 16 * (NX // 2 + 1))
            meet(dve, 2)

            def row_max(m, i, count):
                dve.wait_ge(s_ready, count)
                nc.vector.tensor_reduce(nmax[:, m % 4:m % 4 + 1], score_view(i), AX.X if i < TG else AX.XY,
                                        ALU.max, negate=True).then_inc(max_done, 1)

            def row_recip(m, count):
                dve.wait_ge(exp_done, count)
                nc.vector.reciprocal(rinv[:, m % 4:m % 4 + 1], rsum[:, m % 4:m % 4 + 1]).then_inc(rec_done, 1)

            def add_out(bank, block, ready):
                dve.wait_ge(aux_ready, ready)
                v = acc[:, bass.ts(block, BLK)]
                nc.vector.tensor_tensor(v, ps[:, bank, :], v, ALU.add).then_inc(aux_free, 1)

            def out_lo(h, g, his):
                dve.wait_ge(o_hi, his)
                q = slice(BLK * g, BLK * (g + 1))
                nc.vector.tensor_tensor(o_2[0:HD, h, q], ps[0:HD, O_BANK, :], o_1[0:HD, h, q].bitcast(F32),
                                        ALU.subtract).then_inc(o_lo, 1)

            nc.vector.memset(pT_lo[1][:, :, :].bitcast(F32), 0.0).then_inc(zeroed, 1)
            for m in range(AHEAD):
                row_max(m, m, m + 1)
            row_recip(0, 1)
            row_recip(1, 2)
            for k, free in enumerate((*[t_free] * FREE0, o_hi, o_lo)):
                nc.vector.memset(spare[:, 3 + k:4 + k], 0.0).then_inc(free, 1)
            for it in each_pair(dve):
                for s in range(SLOTS):
                    i, il, g = s % TB, s % TG, s % TB // TG
                    row_recip(s + 2, it * SLOTS + s + 3)
                    if s in EVAC_AT:
                        head, part = EVAC_AT[s]
                        out_lo(head, part, it * 4 + PV_NO[head, part] + 2)
                    for c, (j, nj) in enumerate(chunks(i)):
                        dve.wait_ge(t_hi, it * CHUNKS + chunk_no(s) + c + 1)
                        d = (slice(None), slice(j, j + nj), slice(P * il, P * (il + 1)))
                        nc.vector.tensor_tensor(
                            pT_lo[g][d],
                            ps[:, RING_BANK[chunk_no(s) + c], 0:P * nj].rearrange("p (j q) -> p j q", q=P),
                            pT_hi[g][d].bitcast(F32), ALU.subtract).then_inc(t_free, 1)
                    job = AUX_AT.get(s)
                    if job in ("Y0", "Y1"):
                        half = int(job[1])
                        add_out(RING_BANK[job], (it + STEPS - 1) % STEPS // PAIRS * GB + half, it * AUX + AUX0 + AUX_NO[job] + 1)
                    row_max(s + AHEAD, (s + AHEAD) % TB, it * SLOTS + s + AHEAD + 1)
            out_lo(1, 1, STEPS * 4 + 2)
            for half in range(GB):
                add_out(RING[half], (NB - 1) * GB + half, STEPS * AUX + AUX0 + half + 1)
            dve.wait_ge(ld_res, 16)
            for g in range(NG):
                dve.wait_ge(f_ready, g + 1)
                v = res[:, TG * g:TG * (g + 1), :]
                nc.vector.tensor_tensor(v, ps[:, g % 2, :].rearrange("p (t e) -> p t e", e=P), v, ALU.add
                                        ).then_inc(f_done, 1)

        @block.tensor
        def _(pe):
            pe.wait_ge(made, MADE - 1)
            pe.wait_ge(ld_rows, 5 * 16)
            pe.transpose(ps[:, 5, 0:P], rows[:, :], ident[:, :]).then_inc(rowsT, 1)
            def logits(g):
                pe.wait_ge(x2_f, g + 1)
                for t in range(TG * g, TG * (g + 1)):
                    mm = pe.matmul(ps[:, 4, NX * t:NX * (t + 1)], x2T[:, P * t:P * (t + 1)], wr_sb[:, :],
                                   start=True, stop=True)
                return mm

            pe.wait_ge(ld_wr, 32)
            for g in range(NG):
                pe.wait_ge(x2_rows, g // 2 + 1)
                if g >= 2:
                    pe.wait_ge(x2_f, g - 1)
                for t in range(TG):
                    mm = pe.transpose(ps[:, 2 + g % 2, P * t:P * (t + 1)], sq[:, TG * g + t, :], ident[:, :])
                mm.then_inc(x2_ready, 1)
                if g >= 1:
                    logits(g - 1)
            logits(NG - 1).then_inc(routed, 1)

            def transpose_xn(blocks):
                for g in blocks:
                    if g >= 2:
                        pe.wait_ge(xT_lo, g - 1)
                    for t in range(TG):
                        mm = pe.transpose(ps[:, g % 2, P * t:P * (t + 1)], xs[:, TG * g + t, :], ident[:, :])
                    mm.then_inc(xT_ready, 1)

            transpose_xn(range(EARLY_G))
            pe.wait_ge(b1_relu, 1)
            pe.wait_ge(ld_w2, 16)
            for e in range(NX):
                for f in range(FB):
                    mm = pe.matmul(ps[:, 6, e:e + 1], w2_all[:, e * FB + f, :], relu_b1[:, e * FB + f:e * FB + f + 1],
                                   start=(f == 0), stop=(f == FB - 1))
            mm.then_inc(corr, 1)
            pe.wait_ge(gated_up, 1)
            for k in range(2):
                pe.transpose(ps[:, 7, P * k:P * (k + 1)],
                             gate[:, :, :].rearrange("p e t -> p (e t)")[:, P * k:P * (k + 1)],
                             ident[:, :]).then_inc(gT_ready, 1)
            transpose_xn(range(EARLY_G, NG))
            meet(pe, 1)

            def three(dst, w_hi, w_lo, m_hi, m_lo, start, stop):
                pe.matmul(dst, w_hi, m_hi, start=start, stop=False)
                pe.matmul(dst, w_hi, m_lo, start=False, stop=False)
                return pe.matmul(dst, w_lo, m_hi, start=False, stop=stop)

            def hidden(b, parity, splits, relus):
                pe.wait_ge(w_lo_done, splits)
                s = slice(BLK * b, BLK * (b + 1))
                for f in range(FB):
                    if relus is not None:
                        pe.wait_ge(h_relu, relus + f + 1)
                    c = slice(P * f, P * (f + 1))
                    three(ps[:, f, :], w1_hi[parity][:, c], w1_lo[parity][:, c], x2T_hi[:, s], x2T_lo[:, s],
                          True, True).then_inc(h_ready, 1)

            hidden(0, 0, 2, None)
            with pe.Fori(0, NX // 2) as it:
                for u in range(2 * NG):
                    n = it * (2 * NG) + u
                    ahead = (u + 1) // NG
                    hidden((u + 1) % NG, ahead % 2, it * 4 + 2 * (ahead + 1), n * FB)
                    pe.wait_ge(y_gated, n + 1)
                    for f in range(FB):
                        pe.wait_ge(h_lo, n * FB + f + 1)
                        c = slice(P * f, P * (f + 1))
                        mm = three(ps[:, 4, :], w2_hi[u // NG][:, c], w2_lo[u // NG][:, c],
                                   hid_hi[:, u % 2, f, :], hid_lo[:, u % 2, f, :], f == 0, f == FB - 1)
                    mm.then_inc(y_ready, 1)
            meet(pe, 2)

            def project(bank, slot, block):
                s = bass.ts(block, BLK)
                three(ps[:, bank, :], w_qkv[:, 2 * slot, :], w_qkv[:, 2 * slot + 1, :], xnT_hi[:, s], xnT_lo[:, s],
                      True, True).then_inc(aux_ready, 1)

            def scores(i, h):
                b, n = SCORE_BANK[i], P * (i + 1)
                qt = qq[h][:, P * i:P * (i + 1)]
                halves = [(b, 0, max(n, 2 * P))] if i < TG else [(b, 0, n // 2), (b + 1, n // 2, n // 2)]
                for bank, k0, nk in halves:
                    last = bank == halves[-1][0]
                    pe.matmul(ps[:, bank, 0:nk], qt, kh[h][:, k0:k0 + nk], start=True, stop=False)
                    pe.matmul(ps[:, bank, 0:nk], qt, kl[h][:, k0:k0 + nk], start=False, stop=not last)
                    if last:
                        d = n - k0
                        pe.matmul(ps[:, bank, d - P:d], ident_bf[:, :], causal[:, :], start=False, stop=True
                                  ).then_inc(s_ready, 1)

            def transposes(m, bank, j, nj):
                for k in range(nj):
                    mm = pe.transpose(ps[:, bank, P * k:P * (k + 1)], prb[:, m % 4, P * (j + k):P * (j + k + 1)],
                                      ident[:, :])
                mm.then_inc(t_ready, 1)

            def weighted(h, g, first, end):
                for j in range(first, end):
                    q0 = P * min(max(j - TG * g, 0), TG - 2)
                    last = j == TG * (g + 1) - 1
                    for part, p in enumerate((pT_hi[g], pT_lo[g])):
                        mm = pe.matmul(ps[:, O_BANK, q0:BLK], vv[:, j, h, :], p[:, j, q0:BLK],
                                       start=(j == 0 and part == 0), stop=(last and part == 1))
                if last:
                    mm.then_inc(o_ready, 1)

            def project_out(bank, half):
                q = slice(BLK * half, BLK * (half + 1))
                for h in range(2):
                    pe.matmul(ps[:, bank, :], w_out[:, 2 * h, :], o_1[:, h, q], start=(h == 0), stop=False)
                    mm = pe.matmul(ps[:, bank, :], w_out[:, 2 * h + 1, :], o_2[:, h, q], start=False, stop=(h == 1))
                mm.then_inc(aux_ready, 1)

            pe.wait_ge(ld_qkv, 16)
            for k in range(AUX0):
                if k >= 3:
                    pe.wait_ge(aux_sb, k - 2)
                project(RING[k % 3], k // 2, k % 2)
            pe.wait_ge(qk_in[0], 96)
            for m in range(AHEAD):
                scores(m, 0)
            pe.wait_ge(aux_sb, SPLITS0)
            pe.wait_ge(aux_free, FREES0)
            pe.wait_ge(zeroed, ZEROED)

            def bank_is_read(item, it):
                before, earlier = held_by(item)
                if before in SPLIT_NO:
                    pe.wait_ge(aux_sb, it * SPLITS + SPLITS0 + SPLIT_NO[before] + 1 - (SPLITS if earlier else 0))
                elif before in FREE_NO:
                    pe.wait_ge(aux_free, it * FREES + FREES0 + FREE_NO[before] + 1 - (FREES if earlier else 0))
                else:
                    pe.wait_ge(t_free, it * CHUNKS + FREE0 + before + 1 - (CHUNKS if earlier else 0))

            for it in each_pair(pe):
                next_b = (it + 1) % STEPS // PAIRS * GB
                for s in range(SLOTS):
                    pe.wait_ge(norm_done, it * SLOTS + s + 1)
                    for c, (j, nj) in enumerate(chunks(s % TB)):
                        no = chunk_no(s) + c
                        bank_is_read(no, it)
                        transposes(s, RING_BANK[no], j, nj)
                    job = AUX_AT.get(s)
                    if job:
                        bank_is_read(job, it)
                    if job in ("Q0", "Q1", "K0", "K1", "V0", "V1"):
                        if job == "Q0":
                            pe.wait_ge(ld_qkv, it * 16 + 32)
                        project(RING_BANK[job], "QKV".index(job[0]), next_b + int(job[1]))
                    if job in ("VT0", "VT1"):
                        for k in range(TG):
                            j = TG * int(job[2]) + k
                            mm = pe.transpose(ps[:, RING_BANK[job], P * k:P * (k + 1)], v_st[:, P * j:P * (j + 1)],
                                              ident[:, :])
                        mm.then_inc(aux_ready, 1)
                    if job == "Y0":
                        pe.wait_ge(ld_out, it * 16 + 16)
                        pe.wait_ge(o_dup[0], it * 32 + 16)
                        pe.wait_ge(o_lo, it * 4 + 1)
                        project_out(RING_BANK[job], 0)
                    if job == "Y1":
                        pe.wait_ge(o_dup[1], it * 32 + 16)
                        pe.wait_ge(o_lo, it * 4 + 2)
                        project_out(RING_BANK[job], 1)
                    m = s + AHEAD
                    if m % TB == 0:
                        pe.wait_ge(qk_in[m // TB % 2], it * 96 + 96 * (1 + m // SLOTS))
                    pe.wait_ge(exp_done, it * SLOTS + m + 1 - HELD_BY[m % TB])
                    scores(m % TB, m // TB % 2)
                    if s in PV_AT:
                        h, g, first, end = PV_AT[s]
                        if first == 0:
                            pe.wait_ge(o_lo, it * 4 + PV_NO[h, g] + 1)
                            done = chunk_no(TB * h + TG * (g + 1)) - (CHUNKS if s < TG else 0)
                            pe.wait_ge(t_free, it * CHUNKS + done + FREE0)
                        if (h, g, first) == (0, 0, 0):
                            pe.wait_ge(aux_lo, it * SPLITS + SPLITS0 + SPLIT_NO["VT0"] + 1)
                        if (h, g, first) == (0, 1, 0):
                            pe.wait_ge(aux_lo, it * SPLITS + SPLITS0 + SPLIT_NO["VT1"] + 1)
                        weighted(h, g, first, end)
            pe.wait_ge(o_lo, STEPS * 4 + 1)
            pe.wait_ge(t_free, STEPS * CHUNKS + FREE0)
            weighted(1, 1, 0, TB)
            pe.wait_ge(ld_out, STEPS * 16 + 16)
            for g in range(GB):
                pe.wait_ge(o_dup[g], STEPS * 32 + 16)
            pe.wait_ge(o_lo, STEPS * 4 + 2)
            pe.wait_ge(aux_free, STEPS * FREES + FREES0)
            for half in range(GB):
                project_out(RING[half], half)
            pe.wait_ge(exp_done, STEPS * SLOTS + EXP_AHEAD)
            pe.wait_ge(aux_free, STEPS * FREES + FREES0 + GB)
            for g in range(NG):
                if g >= 2:
                    pe.wait_ge(f_done, g - 1)
                for t in range(TG):
                    mm = pe.transpose(ps[:, g % 2, P * t:P * (t + 1)], acc[:, BLK * g + P * t:BLK * g + P * (t + 1)],
                                      ident[:, :])
                mm.then_inc(f_ready, 1)


_INS = ["L0_attn_x", "L0_attn_w_q", "L0_attn_w_k", "L0_attn_w_v", "L0_attn_w_u", "L0_attn_b_u",
        "L0_ffn_gamma", "L0_ffn_beta", "L0_ffn_Wr", "L0_ffn_br", "L0_ffn_W1", "L0_ffn_b1",
        "L0_ffn_W2", "L0_ffn_b2"]


def kernel(**inputs):
    import numpy as np
    import concourse.bacc as bacc
    from concourse.bass_utils import run_bass_kernel_spmd

    nc = bacc.Bacc("TRN2", target_bir_lowering=False, num_devices=1)
    arrays, args = {}, []
    for name in _INS:
        a = np.ascontiguousarray(inputs[name])
        arrays[f"in_{name}"] = a
        args.append(nc.dram_tensor(f"in_{name}", a.shape, mybir.dt.from_np(a.dtype), kind="ExternalInput").ap())
    shape = arrays["in_L0_attn_x"].shape
    args.append(nc.dram_tensor("out_0", shape, F32, kind="ExternalOutput").ap())
    build(nc, *args)
    r = run_bass_kernel_spmd(nc, [arrays], core_ids=[0])
    return r.results[0]["out_0"]
```
